# Optimizing a Trainium2 kernel written in Bass

```python
import numpy as np
import jax
import jax.numpy as jnp

def _softmax(x, axis=-1):
    return jax.nn.softmax(x, axis=axis)

def _gelu(x):
    return jax.nn.gelu(x, approximate=True)

def _silu(x):
    return jax.nn.silu(x)

def _sigmoid(x):
    return jax.nn.sigmoid(x)

def _layernorm(x, axis=-1, eps=1e-05):
    m = jnp.mean(x, axis=axis, keepdims=True)
    v = jnp.var(x, axis=axis, keepdims=True)
    return (x - m) / jnp.sqrt(v + eps)

def _scatter_add(tgt, idx, src, axis=0):
    return tgt.at[idx].add(src)

def _segment_sum(src, seg, n):
    return jax.ops.segment_sum(src, seg, n)
kernel_name = 'mk_gnn_preln_d2_gnn_r16_6123b6'

def setup_inputs(seed: int=0):
    np.random.seed(seed)
    _w = jnp.asarray

    def _rec_inputs():
        import jax
        import jax.numpy as jnp
        _gk = jax.random.key(seed)
        x = -0.0003713 + 1 * jax.random.normal(jax.random.fold_in(_gk, 1), (3125, 256), jnp.float32)
        src = jax.random.randint(jax.random.fold_in(_gk, 2), (100000,), 0, 3125, jnp.int32)
        dst = jax.random.randint(jax.random.fold_in(_gk, 3), (100000,), 0, 3125, jnp.int32)
        _o = jnp.argsort(dst, stable=True)
        src = src[_o]
        dst = dst[_o]
        edge_weight = jax.random.uniform(jax.random.fold_in(_gk, 12), (100000,), jnp.float32, 0.0, 0.999999)
        return (x, src, dst, edge_weight)
    x, src, dst, edge_weight = _rec_inputs()

    def _L0_gnn_setup():
        import jax, jax.numpy as jnp
        import numpy as np
        N_NODES = 3125
        N_EDGES = 50000
        NODE_DIM = 256
        HIDDEN_DIM = 256
        LN_EPS = 1e-05

        def _spmm(src, dst, w, x, n):
            return jax.ops.segment_sum(w[:, None] * x[src], dst, num_segments=n)

        def _layer_norm(x, g, b):
            mu = jnp.mean(x, -1, keepdims=True)
            var = jnp.mean(jnp.square(x - mu), -1, keepdims=True)
            return (x - mu) * jax.lax.rsqrt(var + LN_EPS) * g + b
        key = jax.random.key(seed)
        ks = jax.random.split(key, 8)
        d, h = (NODE_DIM, HIDDEN_DIM)
        return {'node_features': jax.random.normal(ks[0], (N_NODES, d), jnp.float32), 'src': jax.random.randint(ks[1], (N_EDGES,), 0, N_NODES, jnp.int32), 'dst': jax.random.randint(ks[2], (N_EDGES,), 0, N_NODES, jnp.int32), 'edge_weight': jax.random.uniform(ks[3], (N_EDGES,), jnp.float32), 'W1': jax.random.normal(ks[4], (d, h), jnp.float32) / np.sqrt(d), 'b1': jnp.zeros((h,), jnp.float32), 'g1': jnp.ones((h,), jnp.float32), 'be1': jnp.zeros((h,), jnp.float32), 'W2': jax.random.normal(ks[5], (h, h), jnp.float32) / np.sqrt(h), 'b2': jnp.zeros((h,), jnp.float32), 'g2': jnp.ones((h,), jnp.float32), 'be2': jnp.zeros((h,), jnp.float32), 'Wp': jax.random.normal(ks[6], (h, d), jnp.float32) / np.sqrt(h), 'bp': jnp.zeros((d,), jnp.float32)}
    _L0_gnn_all = _L0_gnn_setup()
    _L0_gnn_in = {k: v for k, v in _L0_gnn_all.items() if k in ('W1', 'b1', 'g1', 'be1', 'W2', 'b2', 'g2', 'be2', 'Wp', 'bp')}
    del _L0_gnn_all

    def _L1_gnn_setup():
        import jax, jax.numpy as jnp
        import numpy as np
        N_NODES = 625
        N_RAND_EDGES = 20000
        IN_DIM = 256
        HIDDEN = 64
        HEADS = 8
        OUT_DIM = 256
        NEG_SLOPE = 0.2

        def gat_conv(x, W, attn_l, attn_r, src, dst, n_nodes):
            H, D = attn_l.shape
            feat = (x @ W).reshape(n_nodes, H, D)
            el = jnp.einsum('nhd,hd->nh', feat, attn_l)
            er = jnp.einsum('nhd,hd->nh', feat, attn_r)
            e = jax.nn.leaky_relu(el[src] + er[dst], NEG_SLOPE)
            m = jax.ops.segment_max(e, dst, num_segments=n_nodes)
            ex = jnp.exp(e - m[dst])
            denom = jax.ops.segment_sum(ex, dst, num_segments=n_nodes)
            alpha = ex / denom[dst]
            out = jax.ops.segment_sum(alpha[:, :, None] * feat[src], dst, num_segments=n_nodes)
            return out.reshape(n_nodes, H * D)
        key = jax.random.key(seed)
        ks = jax.random.split(key, 9)
        h = jax.random.normal(ks[0], (N_NODES, IN_DIM), dtype=jnp.float32)
        src = jnp.concatenate([jax.random.randint(ks[1], (N_RAND_EDGES,), 0, N_NODES, dtype=jnp.int32), jnp.arange(N_NODES, dtype=jnp.int32)])
        dst = jnp.concatenate([jax.random.randint(ks[2], (N_RAND_EDGES,), 0, N_NODES, dtype=jnp.int32), jnp.arange(N_NODES, dtype=jnp.int32)])

        def glorot(k, shape):
            fan = shape[0] + shape[-1]
            s = jnp.sqrt(2.0 / fan).astype(jnp.float32)
            return jax.random.normal(k, shape, dtype=jnp.float32) * s
        W1 = glorot(ks[3], (IN_DIM, HEADS * HIDDEN))
        attn_l1 = glorot(ks[4], (HEADS, HIDDEN))
        attn_r1 = glorot(ks[5], (HEADS, HIDDEN))
        W2 = glorot(ks[6], (HEADS * HIDDEN, OUT_DIM))
        attn_l2 = glorot(ks[7], (1, OUT_DIM))
        attn_r2 = glorot(ks[8], (1, OUT_DIM))
        return {'h': h, 'W1': W1, 'attn_l1': attn_l1, 'attn_r1': attn_r1, 'W2': W2, 'attn_l2': attn_l2, 'attn_r2': attn_r2, 'src': src, 'dst': dst}
    _L1_gnn_all = _L1_gnn_setup()
    _L1_gnn_in = {k: v for k, v in _L1_gnn_all.items() if k in ('W1', 'attn_l1', 'attn_r1', 'W2', 'attn_l2', 'attn_r2')}
    del _L1_gnn_all
    return {'x': x, 'src': src, 'dst': dst, 'edge_weight': edge_weight, 'L0_gnn_W1': _L0_gnn_in['W1'], 'L0_gnn_b1': _L0_gnn_in['b1'], 'L0_gnn_g1': _L0_gnn_in['g1'], 'L0_gnn_be1': _L0_gnn_in['be1'], 'L0_gnn_W2': _L0_gnn_in['W2'], 'L0_gnn_b2': _L0_gnn_in['b2'], 'L0_gnn_g2': _L0_gnn_in['g2'], 'L0_gnn_be2': _L0_gnn_in['be2'], 'L0_gnn_Wp': _L0_gnn_in['Wp'], 'L0_gnn_bp': _L0_gnn_in['bp'], 'L1_gnn_W1': _L1_gnn_in['W1'], 'L1_gnn_attn_l1': _L1_gnn_in['attn_l1'], 'L1_gnn_attn_r1': _L1_gnn_in['attn_r1'], 'L1_gnn_W2': _L1_gnn_in['W2'], 'L1_gnn_attn_l2': _L1_gnn_in['attn_l2'], 'L1_gnn_attn_r2': _L1_gnn_in['attn_r2']}

def reference(x, src, dst, edge_weight, L0_gnn_W1, L0_gnn_b1, L0_gnn_g1, L0_gnn_be1, L0_gnn_W2, L0_gnn_b2, L0_gnn_g2, L0_gnn_be2, L0_gnn_Wp, L0_gnn_bp, L1_gnn_W1, L1_gnn_attn_l1, L1_gnn_attn_r1, L1_gnn_W2, L1_gnn_attn_l2, L1_gnn_attn_r2):
    import jax
    import jax.numpy as jnp

    def _L0_gnn_ref(node_features, src, dst, edge_weight, W1, b1, g1, be1, W2, b2, g2, be2, Wp, bp):
        import jax, jax.numpy as jnp
        import numpy as np
        N_NODES = 3125
        N_EDGES = 50000
        NODE_DIM = 256
        HIDDEN_DIM = 256
        LN_EPS = 1e-05

        def _spmm(src, dst, w, x, n):
            return jax.ops.segment_sum(w[:, None] * x[src], dst, num_segments=n)

        def _layer_norm(x, g, b):
            mu = jnp.mean(x, -1, keepdims=True)
            var = jnp.mean(jnp.square(x - mu), -1, keepdims=True)
            return (x - mu) * jax.lax.rsqrt(var + LN_EPS) * g + b
        n = node_features.shape[0]
        x = node_features
        for W, b, g, be in ((W1, b1, g1, be1), (W2, b2, g2, be2)):
            agg = _spmm(src, dst, edge_weight, x, n)
            h = (x + agg) @ W + b
            x = jax.nn.gelu(_layer_norm(h, g, be), approximate=False)
        return x @ Wp + bp

    def _L1_gnn_ref(h, W1, attn_l1, attn_r1, W2, attn_l2, attn_r2, src, dst):
        import jax, jax.numpy as jnp
        import numpy as np
        N_NODES = 625
        N_RAND_EDGES = 20000
        IN_DIM = 256
        HIDDEN = 64
        HEADS = 8
        OUT_DIM = 256
        NEG_SLOPE = 0.2

        def gat_conv(x, W, attn_l, attn_r, src, dst, n_nodes):
            H, D = attn_l.shape
            feat = (x @ W).reshape(n_nodes, H, D)
            el = jnp.einsum('nhd,hd->nh', feat, attn_l)
            er = jnp.einsum('nhd,hd->nh', feat, attn_r)
            e = jax.nn.leaky_relu(el[src] + er[dst], NEG_SLOPE)
            m = jax.ops.segment_max(e, dst, num_segments=n_nodes)
            ex = jnp.exp(e - m[dst])
            denom = jax.ops.segment_sum(ex, dst, num_segments=n_nodes)
            alpha = ex / denom[dst]
            out = jax.ops.segment_sum(alpha[:, :, None] * feat[src], dst, num_segments=n_nodes)
            return out.reshape(n_nodes, H * D)
        n = h.shape[0]
        x = gat_conv(h, W1, attn_l1, attn_r1, src, dst, n)
        x = jax.nn.elu(x)
        out = gat_conv(x, W2, attn_l2, attn_r2, src, dst, n)
        return out
    h = jnp.maximum(_layernorm(x, axis=-1), 0.0)
    x = x + _L0_gnn_ref(h, src, dst, edge_weight, L0_gnn_W1, L0_gnn_b1, L0_gnn_g1, L0_gnn_be1, L0_gnn_W2, L0_gnn_b2, L0_gnn_g2, L0_gnn_be2, L0_gnn_Wp, L0_gnn_bp)
    h = jnp.maximum(_layernorm(x, axis=-1), 0.0)
    x = x + _L1_gnn_ref(h, L1_gnn_W1, L1_gnn_attn_l1, L1_gnn_attn_r1, L1_gnn_W2, L1_gnn_attn_l2, L1_gnn_attn_r2, src, dst)
    return x

_drawn_inputs = setup_inputs


def setup_inputs(seed=0):
    import zlib

    import numpy as np

    out = dict(_drawn_inputs(seed))
    spreads = {'L0_gnn_b1': (0.0, 0.8),
     'L0_gnn_g1': (1.0, 0.2),
     'L0_gnn_be1': (0.0, 0.1),
     'L0_gnn_b2': (0.0, 0.8),
     'L0_gnn_g2': (1.0, 0.2),
     'L0_gnn_be2': (0.0, 0.1),
     'L0_gnn_bp': (0.0, 0.1)}
    factors = {'L1_gnn_attn_l1': 3.543,
     'L1_gnn_attn_r1': 8.0,
     'L1_gnn_attn_l2': 8.0,
     'L1_gnn_attn_r2': 8.0}
    for name, (base, spread) in spreads.items():
        noise = np.random.default_rng([zlib.crc32(name.encode()), seed]).standard_normal(out[name].shape)
        drawn = base * np.exp(spread * noise) if base else spread * noise
        out[name] = jnp.asarray(drawn.astype(out[name].dtype))
    for name, factor in factors.items():
        out[name] = (out[name] * factor).astype(out[name].dtype)
    return out
```

```python
from contextlib import ExitStack

import concourse.bass as bass
from concourse import mybir

F32 = mybir.dt.float32
I32 = mybir.dt.int32
BF16 = mybir.dt.bfloat16
ALU = mybir.AluOpType
ACT = mybir.ActivationFunctionType
AX = mybir.AxisListType.X

P = 128
N = 3125
NB = 25
NP = NB * P
LAST = N - (NB - 1) * P
E = 100000
CH = 256
NC = 391
EP = NC * CH
J = EP // P
EFULL = (P - 1) * J
NS = E // CH + NB
D = 256
BIG = 1.0e30
EPS = 1e-5


class Eng:

    def __init__(self, sem):
        self.sem, self.n, self.q, self.seen = sem, 0, [], {}

    def need(self, *toks):
        for t in toks:
            if t is None:
                continue
            sem, v = t
            if self.seen.get(id(sem), 0) < v:
                self.seen[id(sem)] = v
                self.q.append(lambda e, sem=sem, v=v: e.wait_ge(sem, v))

    def do(self, f, *toks):
        self.need(*toks)
        self.n += 1
        self.q.append(lambda e: f(e).then_inc(self.sem, 1))
        return self.sem, self.n

    def raw(self, f, *toks):
        self.need(*toks)
        self.q.append(f)

    def replay(self, e):
        for f in self.q:
            f(e)


class Landing:

    def __init__(self, sem):
        self.sem, self.n = sem, 0

    def go(self, eng, f, *toks):
        eng.need(*toks)
        self.n += 16
        eng.q.append(lambda e: f(e).then_inc(self.sem, 16))
        return self.sem, self.n


def program(nc, x, src, dst, ew, w1, b1, g1, be1, w2, b2, g2, be2, wp, bp,
            gw1, al1, ar1, gw2, al2, ar2, out):
    ctx = ExitStack()
    with ctx:
        def sb(name, shape, dt=F32):
            return ctx.enter_context(nc.sbuf_tensor(name, shape, dt))

        def psum(name, shape):
            return ctx.enter_context(nc.psum_tensor(name, shape, F32))

        def sem(name):
            return ctx.enter_context(nc.semaphore(name))

        def dram(name, shape, dt=F32):
            return nc.dram_tensor(name, shape, dt).ap()

        V, T, A, G, S = (Eng(sem(f"s_{n}")) for n in "vtags")
        lands = {}

        def land(name):
            if name not in lands:
                lands[name] = Landing(sem(f"l_{name}"))
            return lands[name]

        t0 = dram("t0", [NP, D])
        t1 = dram("t1", [NP, D])
        t2 = dram("t2", [NP, 2 * D])
        t3 = dram("t3", [NP, D])
        el_d = dram("el_d", [NP, 8])
        el2_d = dram("el2_d", [NP, 1])
        h_d = dram("h_d", [EP, 8])
        h2_d = dram("h2_d", [EP, 1])
        ex_d = dram("ex_d", [NC, P, 16])
        ex2_d = dram("ex2_d", [NC, P, 2])
        es_d = dram("es_d", [NC, CH], I32)
        ed_d = dram("ed_d", [NC, CH], I32)
        edp_d = dram("edp_d", [EP + 2], I32)
        ewt_d = dram("ewt_d", [NC, CH])

        a0 = sb("a0", [P, 13000])
        a1 = sb("a1", [P, NB, D])
        xres = sb("xres", [P, NB, D])
        a3 = sb("a3", [P, 6400])
        src_n = sb("src_n", [P, J], I32)
        dst_n = sb("dst_n", [P, J], I32)
        w_n = a3[:, 1000:1000 + J]
        nh = sb("nh", [P, J])
        negh = sb("negh", [P, J])
        negt = sb("negt", [P, J])
        dl = sb("dl", [P, 2, 512])
        ndl = sb("ndl", [P, 2, 512])
        wsl = sb("wsl", [P, 2, 512])
        srci = sb("srci", [P, 2, 512], I32)
        br = sb("br", [4, P], I32)
        cr = sb("cr", [4, P], I32)
        w1s = sb("w1s", [P, 2, D])
        w2s = sb("w2s", [P, 2, D])
        wps = sb("wps", [P, 2, D])
        gw1s = sb("gw1s", [P, 2, 528])
        gw2s = sb("gw2s", [P, 4, 258])
        vec = sb("vec", [P, 7, D])
        att1 = sb("att1", [P, 2, 512])
        att2 = sb("att2", [P, 2, D])
        iota = sb("iota", [P, P])
        iotab = sb("iotab", [P, P], BF16)
        ident = sb("ident", [P, P])
        ones = sb("ones", [P, P])
        upper = sb("upper", [P, P])
        ioc = sb("ioc", [P, 32])
        sio = sb("sio", [P, 4])
        small = sb("small", [P, 512])
        smalli = sb("smalli", [P, 64], I32)
        ends = sb("ends", [1, 2], I32)
        oh = sb("oh", [P, 4, 2, P])
        oht = sb("oht", [P, 2, P])
        exb = sb("exb", [P, 8, 16])
        yt = sb("yt", [P, 2, 512])
        stat = sb("stat", [P, NB, 6])
        mv = sb("mv", [P, NB, 2])
        rstd = sb("rstd", [P, NB])
        nmr = sb("nmr", [P, NB])
        elr = sb("elr", [P, NB, 16])
        den = sb("den", [P, NB, 8])
        sidx = sb("sidx", [P, NB], I32)
        deg = sb("deg", [P, NB])
        acol = sb("acol", [P, 4])
        ct = sb("ct", [8, 2, P + 1])
        cin = sb("cin", [P, 8])

        big0, big1 = psum("big0", [P, 1024]), psum("big1", [P, 1024])
        pbig = [big0, big1]
        tp = [psum("tp0", [P, 512]), psum("tp1", [P, 512])]
        mp = [psum("mp0", [P, 512]), psum("mp1", [P, 512])]

        def bc(ap, shape):
            return ap.to_broadcast(shape)

        c_i = G.do(lambda e: e.iota(iota[:, :], [[1, P]], base=0, channel_multiplier=0, allow_small_or_imprecise_dtypes=True))
        c_ib = G.do(lambda e: e.iota(iotab[:, :], [[1, P]], base=0, channel_multiplier=0, allow_small_or_imprecise_dtypes=True))
        c_ic = G.do(lambda e: e.iota(ioc[:, :], [[1, 32]], base=0, channel_multiplier=0, allow_small_or_imprecise_dtypes=True))
        c_s = G.do(lambda e: e.iota(sio[:, :], [[P, 4]], base=0, channel_multiplier=1, allow_small_or_imprecise_dtypes=True))
        c_z = G.do(lambda e: e.memset(ident[:, :], 0.0))
        c_id = G.do(lambda e: e.affine_select(out=ident[:, :], in_=ident[:, :], compare_op=ALU.not_equal, fill=1.0, base=0,
                                              pattern=[[-1, P]], channel_multiplier=1), c_z)
        c_on = G.do(lambda e: e.memset(ones[:, :], 1.0))
        c_zu = G.do(lambda e: e.memset(upper[:, :], 0.0))
        c_up = G.do(lambda e: e.affine_select(out=upper[:, :], in_=upper[:, :], compare_op=ALU.is_ge, fill=1.0, base=0,
                                              pattern=[[-1, P]], channel_multiplier=1), c_zu)
        ce = G.do(lambda e: e.memset(ends[:, 0:1], -1))
        ce = G.do(lambda e: e.memset(ends[:, 1:2], 5000), ce)

        m1 = V.do(lambda e: e.memset(dst_n[:, :], 4000))
        m2 = V.do(lambda e: e.memset(src_n[:, :], 0))
        m3 = V.do(lambda e: e.memset(w_n, 0.0))
        m4 = V.do(lambda e: e.memset(xres[:, NB - 1, :], 0.0))

        def nat(t, d, name, dep):
            lt = None
            for lo, p0, pn in ((0, 0, P - 1), (EFULL, P - 1, 1)):
                n = J if pn > 1 else E - EFULL
                lt = land(name).go(S, lambda e, lo=lo, p0=p0, pn=pn, n=n: e.dma_start(
                    t[p0:p0 + pn, 0:n], d[lo:lo + pn * n].rearrange("(p n) -> p n", n=n)), dep)
            return lt

        d_dst = nat(dst_n, dst, "dst", m1)
        half = 12
        d_x = land("x").go(S, lambda e: e.dma_start(xres[:, 0:half, :], x[0:half * P, :].rearrange("(b p) n -> p b n", p=P)))
        d_src = nat(src_n, src, "src", m2)
        d_w = nat(w_n, ew, "w", m3)
        land("x").go(S, lambda e: e.dma_start(xres[:, half:NB - 1, :], x[half * P:(NB - 1) * P, :].rearrange("(b p) n -> p b n", p=P)))
        d_x = land("x").go(S, lambda e: e.dma_start(xres[0:LAST, NB - 1, :], x[(NB - 1) * P:N, :]), m4)
        d_ed = land("ed").go(S, lambda e: e.dma_start(ed_d.rearrange("c k -> (c k)").rearrange("(p n) -> p n", n=J), dst_n[:, :]), d_dst)
        d_es = land("es").go(S, lambda e: e.dma_start(es_d.rearrange("c k -> (c k)").rearrange("(p n) -> p n", n=J), src_n[:, :]), d_src)
        d_ew = land("ewt").go(S, lambda e: e.dma_start(ewt_d.rearrange("c k -> (c k)").rearrange("(p n) -> p n", n=J), w_n), d_w)
        land("edp").go(S, lambda e: e.dma_start(edp_d[1:EP + 1].rearrange("(p n) -> p n", n=J), dst_n[:, :]), d_dst)
        land("edp").go(S, lambda e: e.dma_start(edp_d[0:1].rearrange("(p n) -> p n", n=1), ends[:, 0:1]), ce)
        d_edp = land("edp").go(S, lambda e: e.dma_start(edp_d[EP + 1:EP + 2].rearrange("(p n) -> p n", n=1), ends[:, 1:2]), ce)
        for t, d in ((w1s, w1), (w2s, w2), (wps, wp)):
            d_wt = land("wt").go(S, lambda e, t=t, d=d: e.dma_start(t[:, :, :], d.rearrange("(k p) n -> p k n", p=P)))
        land("wt").go(S, lambda e: e.dma_start(gw1s[:, :, 0:512], gw1.rearrange("(k p) n -> p k n", p=P)))
        land("wt").go(S, lambda e: e.dma_start(gw2s[:, :, 0:D], gw2.rearrange("(k p) n -> p k n", p=P)))
        for i, d in enumerate((b1, g1, be1, b2, g2, be2, bp)):
            land("wt").go(S, lambda e, i=i, d=d: e.dma_start(vec[:, i, :], d.rearrange("(o n) -> o n", o=1).to_broadcast([P, D])))
        for i, d in enumerate((al1, ar1)):
            land("wt").go(S, lambda e, i=i, d=d: e.dma_start(
                att1[:, i, :], d.rearrange("h d -> (h d)").rearrange("(o n) -> o n", o=1).to_broadcast([P, 512])))
        for i, d in enumerate((al2, ar2)):
            d_wt = land("wt").go(S, lambda e, i=i, d=d: e.dma_start(att2[:, i, :], d.to_broadcast([P, D])))

        cnt = small[:, 0:NB]
        junk = a3[:, 0:J]
        c0 = V.do(lambda e: e.memset(cnt, 0.0))
        for b in range(1, NB):
            c0 = V.do(lambda e, b=b: e.tensor_scalar(junk, dst_n[:, :], float(P * b), None, ALU.is_lt, ALU.add,
                                                     accum_out=small[:, b:b + 1]), d_dst, c0)
        eb = T.do(lambda e: e.matmul(tp[0][:, 0:NB], ones[:, :], cnt, start=True, stop=True), c0, c_on)
        v = V.do(lambda e: e.tensor_copy(smalli[:, 0:NB], tp[0][:, 0:NB]), eb)
        v = V.do(lambda e: e.tensor_scalar(smalli[:, 32:32 + NB], smalli[:, 0:NB], 8, None, ALU.arith_shift_right), v)
        v = V.do(lambda e: e.tensor_copy(small[:, 32:32 + NB], smalli[:, 32:32 + NB]), v)
        v = V.do(lambda e: e.tensor_tensor(small[:, 64:64 + NB], small[:, 32:32 + NB], ioc[:, 0:NB], ALU.add), v, c_ic)
        cmp = small[:, 128:128 + 96].rearrange("p (k b) -> p k b", k=4)
        v = V.do(lambda e: e.tensor_tensor(cmp, bc(sio[:, :].rearrange("p (k o) -> p k o", o=1), [P, 4, 24]),
                                           bc(small[:, 65:65 + 24].rearrange("p (o b) -> p o b", o=1), [P, 4, 24]),
                                           ALU.is_ge), v, c_s)
        bs = small[:, 256:260]
        cs = small[:, 260:264]
        nbs = small[:, 264:268]
        v = V.do(lambda e: e.tensor_reduce(bs, cmp, AX, ALU.add), v)
        V.do(lambda e: e.tensor_scalar(nbs, bs, -128.0, None, ALU.mult), v)
        v = V.do(lambda e: e.tensor_tensor(cs, sio[:, :], bs, ALU.subtract), v)
        v = V.do(lambda e: e.tensor_scalar(cs, cs, float(NC - 1), None, ALU.min), v)
        v_ci = V.do(lambda e: e.tensor_copy(smalli[:, 60:64], cs), v)
        rows = {}
        for i, (name, d, dep) in enumerate((("rs", es_d, d_es), ("rd", ed_d, d_ed), ("rw", ewt_d, d_ew))):
            o = a0[:, 1024 * i:1024 * (i + 1)]
            o = o.bitcast(I32) if i < 2 else o
            for k in range(4):
                rows[name] = land(name).go(G, lambda e, o=o, k=k, d=d: e.indirect_dma_start(
                    out=o[:, CH * k:CH * (k + 1)], out_offset=None, in_=d,
                    in_offset=bass.IndirectOffsetOnAxis(ap=smalli[:, 60 + k:61 + k], axis=0)), dep, v_ci)
        rsf = a0[:, 3072:4096]
        rdf = a0[:, 4096:5120]
        v_rs = V.do(lambda e: e.tensor_copy(rsf, a0[:, 0:1024].bitcast(I32)), rows["rs"])
        v_rd = None
        for k in range(4):
            v_rd = V.do(lambda e, k=k: e.tensor_scalar(rdf[:, CH * k:CH * (k + 1)], a0[:, 1024 + CH * k:1024 + CH * (k + 1)].bitcast(I32),
                                                       small[:, 264 + k:265 + k], None, ALU.add), rows["rd"], v)
        w = [None, None, None, None]
        n = 0
        banks = tp + mp
        tabs = []
        for f, dep, tab in ((rsf, v_rs, srci), (rdf, v_rd, dl), (a0[:, 2048:3072], rows["rw"], wsl)):
            for j in range(2):
                bk = banks[n % 4]
                for k in range(4):
                    t = T.do(lambda e, f=f, j=j, k=k, bk=bk: e.transpose(
                        bk[:, P * k:P * (k + 1)], f[:, CH * k + j:CH * (k + 1):2], ident[:, :]), dep, c_id, w[n % 4], v)
                w[n % 4] = V.do(lambda e, tab=tab, j=j, bk=bk: e.tensor_copy(tab[:, j, :], bk[:, :]), t)
                tabs.append(w[n % 4])
                n += 1
        v_tab = tabs[-1]
        v_ndl = V.do(lambda e: e.tensor_scalar(ndl[:, :, :], dl[:, :, :], -1.0, None, ALU.mult), v_tab)
        for i, (q, tab) in enumerate(((bs, br), (cs, cr))):
            t = T.do(lambda e, q=q, i=i: e.transpose(banks[i][0:4, 0:P], q, ident[:, :]), v_tab)
            v_reg = V.do(lambda e, i=i, tab=tab: e.tensor_copy(tab[:, :], banks[i][0:4, 0:P]), t)

        def stats(b, ap, *deps):
            s = V.do(lambda e: e.bn_stats(stat[:, b, :], ap), *deps)
            return V.do(lambda e: e.bn_aggr(mv[:, b, :], stat[:, b, :]), s)

        def scales(dep):
            s = V.do(lambda e: e.tensor_scalar(nmr[:, :], mv[:, :, 1], EPS, None, ALU.add), dep)
            s = A.do(lambda e: e.activation(rstd[:, :], nmr[:, :], ACT.Sqrt), s)
            s = V.do(lambda e: e.reciprocal(rstd[:, :], rstd[:, :]), s)
            s = V.do(lambda e: e.tensor_tensor(nmr[:, :], mv[:, :, 0], rstd[:, :], ALU.mult), s)
            return V.do(lambda e: e.tensor_scalar(nmr[:, :], nmr[:, :], -1.0, None, ALU.mult), s)

        def norm(b, o, i, func, *deps):
            return A.do(lambda e: e.activation(o, i, func, bias=nmr[:, b:b + 1], scale=rstd[:, b:b + 1]), *deps)

        GRP = 5

        def store(t, name, b, tok):
            if b % GRP == GRP - 1:
                return land(name).go(S, lambda e: e.dma_start(
                    t[(b - GRP + 1) * P:(b + 1) * P, :].rearrange("(b p) n -> p b n", p=P), a1[:, b - GRP + 1:b + 1, :]), tok)
            return None

        for b in range(NB):
            v = stats(b, xres[:, b, :], d_x)
        v = scales(v)
        for b in range(NB):
            a = norm(b, a1[:, b, :], xres[:, b, :], ACT.Relu, v)
            tab_ready = store(t0, "t0", b, a) or None

        NR = 6
        ring_free = [None] * 8
        oh_free = [None] * 4
        ps_free = [None, None]
        ex_free = [None] * 8
        regs = {}

        def block_of(e, s):
            if s % 4 == 0:
                if "b" not in regs:
                    regs["b"] = [e.alloc_register(f"rb{i}") for i in range(4)]
                k = s // P
                e.load(regs["b"], br[k:k + 1, s % P:s % P + 4])
            return e.snap(regs["b"][s % 4], min_val=0, max_val=NB - 1)

        def chunk_of(e, s):
            if s % 4 == 0:
                if "c" not in regs:
                    regs["c"] = [e.alloc_register(f"rc{i}") for i in range(4)]
                k = s // P
                e.load(regs["c"], cr[k:k + 1, s % P:s % P + 4])
            return e.snap(regs["c"][s % 4], min_val=0, max_val=NC - 1)

        def aggregate(name, table, mode, acc, start, side=None):
            F = 512 if mode == "heads" else 256
            W = {"weights": 256, "heads": 520, "one": 257}[mode]
            nr = NR
            exd = {"heads": ex_d, "one": ex2_d}.get(mode)
            ew_ = 16 if mode == "heads" else 2
            pend = None
            done = start
            for s in range(NS):
                r = s % nr
                buf = [a3[:, (2 * r + k) * 512:(2 * r + k) * 512 + F] for k in range(2)]
                if exd is not None:
                    q = s % 8
                    x_in = land(f"ex{q}").go(S, lambda e, s=s, q=q: e.dma_start(
                        exb[:, q, 0:ew_], exd[bass.ds(chunk_of(e, s), 1), :, :].rearrange("o p f -> (o p) f")), ex_free[q], start, v_reg)
                for k in range(2):
                    g_in = land(f"g{r}").go(G, lambda e, s=s, k=k, buf=buf: e.indirect_dma_start(
                        out=buf[k], out_offset=None, in_=table,
                        in_offset=bass.IndirectOffsetOnAxis(ap=srci[:, k, s:s + 1], axis=0)), ring_free[r], start, v_tab)
                so = s % 4
                oks = []
                for k in range(2):
                    o = oh[:, so, k, :]
                    if mode == "heads":
                        a = A.do(lambda e, s=s, k=k: e.activation(oht[:, k, :], iota[:, :], ACT.Abs, bias=ndl[:, k, s:s + 1]),
                                 v_ndl, c_i, oh_free[so])
                        ok = A.do(lambda e, k=k, o=o: e.activation(o, oht[:, k, :], ACT.Relu, bias=1.0, scale=-1.0), a)
                    else:
                        sc = wsl[:, k, s:s + 1] if mode == "weights" else exb[:, s % 8, k:k + 1]
                        ok = V.do(lambda e, s=s, k=k, o=o, sc=sc: e.tensor_scalar(o, iota[:, :], dl[:, k, s:s + 1], sc, ALU.is_equal, ALU.mult),
                                  v_tab, c_i, oh_free[so], x_in if exd is not None else None)
                    oks.append(ok)
                if mode == "heads":
                    for k in range(2):
                        bv = buf[k].rearrange("p (h d) -> p h d", h=8)
                        mk = V.do(lambda e, k=k, bv=bv, s=s: e.tensor_tensor(
                            bv, bv, bc(exb[:, s % 8, 8 * k:8 * k + 8].rearrange("p (h o) -> p h o", o=1), [P, 8, 64]), ALU.mult), g_in, x_in)
                        oks.append(mk)
                if pend is not None:
                    done = pend()
                pp = pbig[s % 2]
                t = None
                for k in range(2):
                    t = T.do(lambda e, pp=pp, so=so, k=k, buf=buf: e.matmul(pp[:, 0:F], oh[:, so, k, :], buf[k], start=(k == 0), stop=(k == 1)),
                             *oks, g_in, ps_free[s % 2])
                if mode != "weights":
                    for k in range(2):
                        rhs = exb[:, s % 8, 8 * k:8 * k + 8] if mode == "heads" else ones[:, 0:1]
                        off = 512 if mode == "heads" else 256
                        t = T.do(lambda e, pp=pp, so=so, k=k, rhs=rhs, off=off: e.matmul(
                            pp[:, 512:512 + W - off], oh[:, so, k, :], rhs, start=(k == 0), stop=(k == 1)), x_in)
                ring_free[r] = t
                oh_free[so] = t
                if exd is not None:
                    ex_free[s % 8] = t

                def evac(s=s, t=t, pp=pp):
                    def add(e):
                        b = block_of(e, s)
                        d = acc[:, bass.ds(b * W, W)]
                        if mode == "one":
                            d = acc[:, bass.ds(b * W, 256)]
                            return e.tensor_tensor(d, d, pp[:, 0:256], ALU.add)
                        return e.tensor_tensor(d, d, pp[:, 0:W], ALU.add)
                    tok = V.do(add, t, done, v_reg)
                    if mode == "one":
                        def add2(e):
                            b = e.snap(regs["b"][s % 4], min_val=0, max_val=NB - 1)
                            d = acc[:, bass.ds(b * W + 256, 1)]
                            return e.tensor_tensor(d, d, pp[:, 512:513], ALU.add)
                        tok = V.do(add2)
                    ps_free[s % 2] = tok
                    return tok
                pend = evac
                if side is not None:
                    side(s)
            return pend()

        dn = [0]
        tfree, mfree, yfree = [None, None], [None, None], [None, None]

        def dense(inp, K, ws, Nc, dep, extra=0):
            i = dn[0] % 2
            dn[0] += 1
            for k in range(K):
                t = T.do(lambda e, k=k: e.transpose(tp[i][:, P * k:P * (k + 1)], inp[:, P * k:P * (k + 1)], ident[:, :]),
                         dep, c_id, tfree[i])
            c = A.do(lambda e: e.activation(yt[:, i, 0:P * K], tp[i][:, 0:P * K], ACT.Copy), t, yfree[i])
            tfree[i] = c
            for k in range(K):
                t = T.do(lambda e, k=k: e.matmul(mp[i][:, 0:Nc], yt[:, i, P * k:P * (k + 1)], ws[:, k, 0:Nc],
                                                 start=(k == 0), stop=(k == K - 1)), c, d_wt, mfree[i])
            if extra:
                for k in range(K):
                    t = T.do(lambda e, k=k: e.matmul(pbig[i][:, 0:extra], yt[:, i, P * k:P * (k + 1)], ws[:, k, Nc:Nc + extra],
                                                     start=(k == 0), stop=(k == K - 1)))
            yfree[i] = t
            return i, t

        a1f = a1[:, :, :].rearrange("p b n -> p (b n)")
        hb = a0[:, 6400:12800].rearrange("p (b n) -> p b n", n=D)

        lo = a0[:, 0:J]
        hi = a0[:, 800:800 + J]
        dti = a0[:, 1600:1600 + J].bitcast(I32)
        ohl = a0[:, 2400:2400 + 2 * 1024].bitcast(BF16).rearrange("p (u j d) -> p u j d", u=2, j=16)
        ohh = a0[:, 5000:5000 + 2 * 256].bitcast(BF16).rearrange("p (u j d) -> p u j d", u=2, j=16)
        hst = {"free": [None, None], "t": None}

        def bits():
            v = V.do(lambda e: e.tensor_scalar(dti, dst_n[:, :], 127, None, ALU.bitwise_and), v_reg)
            v = V.do(lambda e: e.tensor_copy(lo, dti), v)
            v = V.do(lambda e: e.tensor_scalar(dti, dst_n[:, :], 7, None, ALU.arith_shift_right), v)
            hst["v"] = V.do(lambda e: e.tensor_copy(hi, dti), v)

        def histogram(s):
            if s % 8 != 4 or s // 8 >= 49:
                return
            g = s // 8
            j0, jn = 16 * g, min(16, J - 16 * g)
            u = g % 2
            v1 = V.do(lambda e: e.tensor_tensor(ohl[:, u, 0:jn, :], bc(iotab[:, :].rearrange("p (o d) -> p o d", o=1), [P, jn, P]),
                                                bc(lo[:, j0:j0 + jn].rearrange("p (j o) -> p j o", o=1), [P, jn, P]), ALU.is_equal),
                      c_ib, hst["v"], hst["free"][u])
            v2 = V.do(lambda e: e.tensor_tensor(ohh[:, u, 0:jn, 0:NB], bc(iotab[:, 0:NB].rearrange("p (o d) -> p o d", o=1), [P, jn, NB]),
                                                bc(hi[:, j0:j0 + jn].rearrange("p (j o) -> p j o", o=1), [P, jn, NB]), ALU.is_equal))
            for i in range(jn):
                t = T.do(lambda e, i=i: e.matmul(mp[0][:, 0:NB], ohl[:, u, i, :], ohh[:, u, i, 0:NB],
                                                 start=(j0 + i == 0), stop=(j0 + i == J - 1)), v2)
            hst["free"][u] = hst["t"] = t

        bits()
        d_t0 = land("t0").sem, land("t0").n
        tok = aggregate("l0", t0, "weights", a1f, d_t0, histogram)

        v = V.do(lambda e: e.tensor_copy(deg[:, :], mp[0][:, 0:NB]), hst["t"])
        t = T.do(lambda e: e.matmul(tp[0][:, 0:NB], ones[:, :], deg[:, :], start=True, stop=True), v)
        t = T.do(lambda e: e.matmul(tp[1][:, 0:NB], upper[:, :], deg[:, :], start=True, stop=True), c_up)
        v = V.do(lambda e: e.tensor_copy(small[:, 0:NB], tp[0][:, 0:NB]), t)
        v = V.do(lambda e: e.tensor_tensor_scan(small[:, 32:32 + NB], ones[:, 0:NB], small[:, 0:NB], 0.0, ALU.mult, ALU.add), v)
        v = V.do(lambda e: e.tensor_tensor(small[:, 64:64 + NB], small[:, 32:32 + NB], small[:, 0:NB], ALU.subtract), v)
        v = V.do(lambda e: e.tensor_tensor(small[:, 64:64 + NB], small[:, 64:64 + NB], tp[1][:, 0:NB], ALU.add), v)
        v = V.do(lambda e: e.tensor_scalar(small[:, 96:96 + NB], deg[:, :], 0.0, 1.0e6, ALU.is_equal, ALU.mult), v)
        v = V.do(lambda e: e.tensor_tensor(small[:, 64:64 + NB], small[:, 64:64 + NB], small[:, 96:96 + NB], ALU.add), v)
        v_sidx = V.do(lambda e: e.tensor_copy(sidx[:, :], small[:, 64:64 + NB]), v)
        tfree[0] = tfree[1] = mfree[0] = v_sidx

        def conv_dense(tok, ws, ib, last):
            for b in range(NB):
                i, t = dense(a1[:, b, :], 2, ws, D, tok)
                v = V.do(lambda e, i=i, b=b: e.tensor_tensor(hb[:, b, :], mp[i][:, 0:D], vec[:, ib, :], ALU.add), t)
                mfree[i] = v
                v = stats(b, hb[:, b, :], v)
            v = scales(v)
            toks = []
            for b in range(NB):
                a = norm(b, hb[:, b, :], hb[:, b, :], ACT.Identity, v)
                g = V.do(lambda e, b=b: e.tensor_tensor(hb[:, b, :], hb[:, b, :], vec[:, ib + 1, :], ALU.mult), a)
                toks.append(V.do(lambda e, b=b: e.tensor_tensor(hb[:, b, :], hb[:, b, :], vec[:, ib + 2, :], ALU.add), g))
            outs = []
            for b in range(NB):
                outs.append(A.do(lambda e, b=b: e.activation(a1[:, b, :], hb[:, b, :], ACT.Gelu), toks[b]))
                if last is not None:
                    store(last, "t1", b, outs[-1])
            return outs

        conv_dense(tok, w1s, 0, t1)
        d_t1 = land("t1").sem, land("t1").n

        dpn = a0[:, 0:J].bitcast(I32)
        dnn = a0[:, 800:800 + J].bitcast(I32)

        def flags():
            land("dp").go(S, lambda e: e.dma_start(dpn, edp_d[0:EP].rearrange("(p n) -> p n", n=J)), d_edp, tok)
            l = land("dp").go(S, lambda e: e.dma_start(dnn, edp_d[2:EP + 2].rearrange("(p n) -> p n", n=J)), d_edp, tok)
            V.do(lambda e: e.tensor_tensor(nh[:, :], dst_n[:, :], dpn, ALU.is_equal), l)
            v = V.do(lambda e: e.tensor_tensor(negt[:, :], dst_n[:, :], dnn, ALU.is_equal))
            V.do(lambda e: e.tensor_scalar(negh[:, :], nh[:, :], BIG, -BIG, ALU.mult, ALU.add), v)
            v = V.do(lambda e: e.tensor_scalar(negt[:, :], negt[:, :], BIG, -BIG, ALU.mult, ALU.add), v)
            for i, q in enumerate((nh, negh, negt)):
                v2 = V.do(lambda e, i=i, q=q: e.tensor_reduce(acol[:, i:i + 1], q[:, :], AX, ALU.min), v)
            return v2

        v_fl = flags()
        z = V.do(lambda e: e.memset(a3[:, :], 0.0), tok)
        land("hz").go(S, lambda e: e.dma_start(h_d.rearrange("e h -> (e h)").rearrange("(p n) -> p n", p=P), a3[:, 0:J * 8]), z)
        d_hz = land("hz").go(S, lambda e: e.dma_start(h2_d.rearrange("e h -> (e h)").rearrange("(p n) -> p n", p=P), a3[:, 0:J]), z)
        ring_free[0:NR] = [d_hz] * NR

        f = v_fl
        for k in range(2):
            for i in range(2):
                f = V.do(lambda e, k=k, i=i: e.tensor_tensor(a0[:, 2000:2512], gw1s[:, k, 0:512], att1[:, i, :], ALU.mult), d_wt, f)
                f = V.do(lambda e, k=k, i=i: e.tensor_reduce(gw1s[:, k, 512 + 8 * i:520 + 8 * i],
                                                             a0[:, 2000:2512].rearrange("p (h d) -> p h d", h=8), AX, ALU.add), f)
        for k in range(4):
            for i in range(2):
                f = V.do(lambda e, k=k, i=i: e.tensor_tensor(a0[:, 2000:2256], gw2s[:, k, 0:D], att2[:, i, :], ALU.mult), f)
                f = V.do(lambda e, k=k, i=i: e.tensor_reduce(gw2s[:, k, D + i:D + i + 1], a0[:, 2000:2256], AX, ALU.add), f)
        v_fold = f

        tok = aggregate("l1", t1, "weights", a1f, d_t1)
        outs = conv_dense(tok, w2s, 3, None)
        for b in range(NB):
            i, t = dense(a1[:, b, :], 2, wps, D, outs[b])
            v = V.do(lambda e, i=i, b=b: e.tensor_tensor(hb[:, b, :], mp[i][:, 0:D], vec[:, 6, :], ALU.add), t)
            mfree[i] = v
            v = V.do(lambda e, b=b: e.tensor_tensor(xres[:, b, :], xres[:, b, :], hb[:, b, :], ALU.add), v)
            v = stats(b, xres[:, b, :], v)
        v = scales(v)
        stage = a3[:, 0:2048].rearrange("p (u n) -> p u n", n=512)
        sfree = [None] * 4
        for b in range(NB):
            a = norm(b, a1[:, b, :], xres[:, b, :], ACT.Relu, v)
            i, t = dense(a1[:, b, :], 2, gw1s, 512, a, 16)
            T.need(v_fold)
            u = b % 4
            c = V.do(lambda e, i=i, u=u: e.tensor_copy(stage[:, u, :], mp[i][:, :]), t, sfree[u])
            c = V.do(lambda e, i=i, b=b: e.tensor_copy(elr[:, b, :], pbig[i][:, 0:16]))
            mfree[i] = c
            sfree[u] = land(f"st{u}").go(S, lambda e, b=b, u=u: e.dma_start(t2[b * P:(b + 1) * P, :], stage[:, u, :]), c)
        d_el = land("el").go(S, lambda e: e.dma_start(el_d.rearrange("(b p) h -> p b h", p=P), elr[:, :, 0:8]), c)
        t2_ready = list(sfree)
        for u in range(4):
            ring_free[u] = sfree[u]

        def carry(lcol, acolumn, H, op0, op1, init, back, dep):
            t = T.do(lambda e: e.transpose(tp[0][0:H, 0:P], lcol, ident[:, :]), dep)
            t = T.do(lambda e: e.transpose(tp[1][0:H, 0:P], bc(acolumn, [P, H]), ident[:, :]), v_fl)
            v = V.do(lambda e: e.tensor_copy(ct[0:H, 0, 0:P], tp[1][0:H, 0:P]), t)
            v = V.do(lambda e: e.memset(ct[0:H, 1, :], init), v)
            if not back:
                v = V.do(lambda e: e.tensor_tensor_scan(ct[0:H, 1, 1:P + 1], ct[0:H, 0, 0:P], tp[0][0:H, 0:P], init, op0, op1), v)
                c = ct[0:H, 1, 0:P]
            else:
                v = V.do(lambda e: e.tensor_tensor_scan(ct[0:H, 1, 0:P][:, ::-1], ct[0:H, 0, 0:P][:, ::-1],
                                                        tp[0][0:H, 0:P][:, ::-1], init, op0, op1), v)
                c = ct[0:H, 1, 1:P + 1]
            t = T.do(lambda e: e.transpose(tp[0][:, 256:256 + H], c, ident[0:H, 0:H]), v)
            return V.do(lambda e: e.tensor_copy(cin[:, 0:H], tp[0][:, 256:256 + H]), t)

        def scan(H, o, i, f, ac, op0, op1, init, back, dep):
            st = -1 if back else 1
            v = dep
            for first in (True, False):
                for h in range(H):
                    ini = init if first else cin[:, h:h + 1]
                    vv = V.do(lambda e, h=h, ini=ini: e.tensor_tensor_scan(
                        o[:, :, h][:, ::st], f[:, ::st], i[:, :, h][:, ::st], ini, op0, op1), v)
                v = vv
                if first:
                    edge = 0 if back else J - 1
                    v = carry(o[:, edge, :], ac, H, op0, op1, init, back, v)
            return v

        def attention(H, eld, elsem, er_sb, hd, exd_flat, dep):
            elv = a0[:, 0:J * H].rearrange("p (j h) -> p j h", h=H)
            erv = a0[:, 6400:6400 + J * H].rearrange("p (j h) -> p j h", h=H)
            fv = a1f[:, 0:J * H].rearrange("p (j h) -> p j h", h=H)
            mvv = a3[:, 0:J * H].rearrange("p (j h) -> p j h", h=H)
            flat = [q for q in (a0[:, 0:J * H], a0[:, 6400:6400 + J * H], a1f[:, 0:J * H], a3[:, 0:J * H])]
            for b in range(NB):
                d = land(f"sc{H}").go(G, lambda e, b=b: e.indirect_dma_start(
                    out=hd, out_offset=bass.IndirectOffsetOnAxis(ap=sidx[:, b:b + 1], axis=0), in_=er_sb(b), in_offset=None,
                    bounds_check=EP - 1, oob_is_err=False), dep, v_sidx, d_hz)
            l = land(f"hl{H}").go(S, lambda e: e.dma_start(flat[1], hd.rearrange("e h -> (e h)").rearrange("(p n) -> p n", p=P)), d)
            for j in range(J):
                g = land(f"eg{H}").go(G, lambda e, j=j: e.indirect_dma_start(
                    out=elv[:, j, :], out_offset=None, in_=eld,
                    in_offset=bass.IndirectOffsetOnAxis(ap=src_n[:, j:j + 1], axis=0)), elsem)
            v = scan(H, mvv, erv, nh, acol[:, 0:1], ALU.mult, ALU.add, 0.0, False, l)
            v = scan(H, fv, elv, negh, acol[:, 1:2], ALU.add, ALU.max, -BIG, False, (V.need(g), v)[1])
            v = scan(H, erv, fv, negt, acol[:, 2:3], ALU.add, ALU.max, -BIG, True, v)
            v = V.do(lambda e: e.tensor_tensor(flat[1], flat[1], flat[3], ALU.add), v)
            v = V.do(lambda e: e.scalar_tensor_tensor(out=flat[1], in0=flat[1], scalar=0.2, in1=flat[1], op0=ALU.mult, op1=ALU.max), v)
            v = V.do(lambda e: e.tensor_tensor(flat[0], flat[0], flat[3], ALU.add), v)
            v = V.do(lambda e: e.scalar_tensor_tensor(out=flat[0], in0=flat[0], scalar=0.2, in1=flat[0], op0=ALU.mult, op1=ALU.max), v)
            v = V.do(lambda e: e.tensor_tensor(flat[0], flat[0], flat[1], ALU.subtract), v)
            a = A.do(lambda e: e.activation(flat[2], flat[0], ACT.Exp), v)
            return land(f"exs{H}").go(S, lambda e: e.dma_start(exd_flat, flat[2]), a), a

        d_ex, a = attention(8, el_d, d_el, lambda b: elr[:, b, 8:16], h_d,
                            ex_d.rearrange("c p f -> (c p f)").rearrange("(p n) -> p n", p=P), c)
        acc1 = a0[:, :]
        z = V.do(lambda e: e.memset(acc1, 0.0), a)
        G.need(a, *t2_ready)
        for i in range(2):
            ps_free[i] = mfree[i]
        tok = aggregate("g1", t2, "heads", acc1, d_ex)
        a13 = acc1.rearrange("p (b w) -> p b w", w=520)
        rden = a1f[:, 0:200].rearrange("p (b h) -> p b h", h=8)
        v = V.do(lambda e: e.tensor_scalar(den[:, :, :], a13[:, :, 512:520], 1e-30, None, ALU.max), tok)
        v = V.do(lambda e: e.reciprocal(den[:, :, :], den[:, :, :]), v)
        t3_st = a1
        etmp = a3[:, 0:4096].rearrange("p (u n) -> p u n", n=512)
        v0 = v
        for b in range(NB):
            u = 2 * (b % 4)
            blk = a13[:, b, 0:512].rearrange("p (h d) -> p h d", h=8)
            v = V.do(lambda e, b=b, blk=blk: e.tensor_tensor(blk, blk, bc(den[:, b, :].rearrange("p (h o) -> p h o", o=1), [P, 8, 64]), ALU.mult), v0)
            v = V.do(lambda e, b=b, u=u: e.tensor_scalar(etmp[:, u, :], a13[:, b, 0:512], 0.0, None, ALU.min), v)
            a = A.do(lambda e, u=u: e.activation(etmp[:, u + 1, :], etmp[:, u, :], ACT.Exp), v)
            v = V.do(lambda e, b=b: e.tensor_scalar(a13[:, b, 0:512], a13[:, b, 0:512], 0.0, -1.0, ALU.max, ALU.add), v)
            v = V.do(lambda e, b=b, u=u: e.tensor_tensor(a13[:, b, 0:512], a13[:, b, 0:512], etmp[:, u + 1, :], ALU.add), a, v)
            i, t = dense(a13[:, b, 0:512], 4, gw2s, D, v, 2)
            c = V.do(lambda e, i=i, b=b: e.tensor_copy(a1[:, b, :], mp[i][:, 0:D]), t)
            c = V.do(lambda e, i=i, b=b: e.tensor_copy(elr[:, b, 0:2], pbig[i][:, 0:2]))
            mfree[i] = c
            store(t3, "t3", b, c)
        d_t3 = land("t3").sem, land("t3").n
        d_el2 = land("el2").go(S, lambda e: e.dma_start(el2_d.rearrange("(b p) h -> p b h", p=P), elr[:, :, 0:1], allow_slow_non_contiguous=True), c)
        V.need(d_t3)
        G.need(c)
        d_ex2, a = attention(1, el2_d, d_el2, lambda b: elr[:, b, 1:2], h2_d,
                             ex2_d.rearrange("c p f -> (c p f)").rearrange("(p n) -> p n", p=P), c)
        acc2 = a0[:, 0:NB * 257]
        z = V.do(lambda e: e.memset(acc2, 0.0), a)
        G.need(a)
        for i in range(2):
            ps_free[i] = mfree[i]
        S.need(d_t3)
        G.need(d_t3)
        tok = aggregate("g2", t3, "one", acc2, d_ex2)
        a23 = acc2.rearrange("p (b w) -> p b w", w=257)
        v = V.do(lambda e: e.tensor_scalar(deg[:, :], a23[:, :, 256], 1e-30, None, ALU.max), tok)
        v = V.do(lambda e: e.reciprocal(deg[:, :], deg[:, :]), v)
        v0 = v
        for b in range(NB):
            v = V.do(lambda e, b=b: e.scalar_tensor_tensor(out=a1[:, b, :], in0=a23[:, b, 0:D], scalar=deg[:, b:b + 1], in1=xres[:, b, :],
                                                           op0=ALU.mult, op1=ALU.add), v0)
            if b < NB - 1 and b % 6 == 5:
                land("out").go(S, lambda e, b=b: e.dma_start(out[(b - 5) * P:(b + 1) * P, :].rearrange("(b p) n -> p b n", p=P),
                                                             a1[:, b - 5:b + 1, :]), v)
        fin = land("out").go(S, lambda e: e.dma_start(out[(NB - 1) * P:N, :], a1[0:LAST, NB - 1, :]), v)
        S.need(fin)

        block = ctx.enter_context(nc.Block())

        @block.sync
        def _(e):
            S.replay(e)

        @block.gpsimd
        def _(e):
            G.replay(e)

        @block.scalar
        def _(e):
            A.replay(e)

        @block.vector
        def _(e):
            V.replay(e)

        @block.tensor
        def _(e):
            T.replay(e)


_INS = ["x", "src", "dst", "edge_weight", "L0_gnn_W1", "L0_gnn_b1", "L0_gnn_g1", "L0_gnn_be1", "L0_gnn_W2", "L0_gnn_b2",
        "L0_gnn_g2", "L0_gnn_be2", "L0_gnn_Wp", "L0_gnn_bp", "L1_gnn_W1", "L1_gnn_attn_l1", "L1_gnn_attn_r1", "L1_gnn_W2",
        "L1_gnn_attn_l2", "L1_gnn_attn_r2"]
_OUTS = [((N, D), "float32")]


def kernel(**inputs):
    import numpy as _np
    import concourse.bacc as _bacc
    from concourse import mybir as _mybir
    from concourse.bass_utils import run_bass_kernel_spmd as _run

    nc = _bacc.Bacc("TRN2", target_bir_lowering=False, num_devices=1)
    arrays, args = {}, []
    for name in _INS:
        a = _np.ascontiguousarray(inputs[name])
        arrays[f"in_{name}_dram"] = a
        args.append(nc.dram_tensor(f"in_{name}_dram", a.shape, _mybir.dt.from_np(a.dtype), kind="ExternalInput").ap())
    for i, (shape, dtype) in enumerate(_OUTS):
        dt = _mybir.dt.from_np(_np.dtype(dtype))
        args.append(nc.dram_tensor(f"out_{i}_dram", shape, dt, kind="ExternalOutput").ap())
    program(nc, *args)
    r = _run(nc, [arrays], core_ids=[0])
    got = tuple(r.results[0][f"out_{i}_dram"] for i in range(len(_OUTS)))
    return got[0]
```

```python
from contextlib import ExitStack

import concourse.bass as bass
from concourse import mybir

F32 = mybir.dt.float32
I32 = mybir.dt.int32
BF16 = mybir.dt.bfloat16
ALU = mybir.AluOpType
ACT = mybir.ActivationFunctionType
AX = mybir.AxisListType.X

P = 128
N = 3125
NB = 25
NP = NB * P
LAST = N - (NB - 1) * P
E = 100000
CH = 256
NC = 391
EP = NC * CH
J = EP // P
EFULL = (P - 1) * J
NS = E // CH + NB
NG = (J + 15) // 16
D = 256
BIG = 1.0e30
EPS = 1e-5


class Eng:

    def __init__(self, sem):
        self.sem, self.n, self.q, self.seen = sem, 0, [], {}

    def need(self, *toks):
        for t in toks:
            if t is None:
                continue
            sem, v = t
            if self.seen.get(id(sem), 0) < v:
                self.seen[id(sem)] = v
                self.q.append(lambda e, sem=sem, v=v: e.wait_ge(sem, v))

    def do(self, f, *toks):
        self.need(*toks)
        self.n += 1
        self.q.append(lambda e: f(e).then_inc(self.sem, 1))
        return self.sem, self.n

    def raw(self, f, *toks):
        self.need(*toks)
        self.q.append(f)

    def replay(self, e):
        for f in self.q:
            f(e)


class Landing:

    def __init__(self, sem):
        self.sem, self.n = sem, 0

    def go(self, eng, f, *toks):
        eng.need(*toks)
        self.n += 16
        eng.q.append(lambda e: f(e).then_inc(self.sem, 16))
        return self.sem, self.n


def program(nc, x, src, dst, ew, w1, b1, g1, be1, w2, b2, g2, be2, wp, bp,
            gw1, al1, ar1, gw2, al2, ar2, out):
    ctx = ExitStack()
    with ctx:
        def sb(name, shape, dt=F32):
            return ctx.enter_context(nc.sbuf_tensor(name, shape, dt))

        def psum(name, shape):
            return ctx.enter_context(nc.psum_tensor(name, shape, F32))

        def sem(name):
            return ctx.enter_context(nc.semaphore(name))

        def dram(name, shape, dt=F32):
            return nc.dram_tensor(name, shape, dt).ap()

        V, T, A, G, S = (Eng(sem(f"s_{n}")) for n in "vtags")
        lands = {}

        def land(name):
            if name not in lands:
                lands[name] = Landing(sem(f"l_{name}"))
            return lands[name]

        t0 = dram("t0", [NP, D])
        t1 = dram("t1", [NP, D])
        t2 = dram("t2", [NP, 2 * D])
        t3 = dram("t3", [NP, D])
        el_d = dram("el_d", [NP, 8])
        el2_d = dram("el2_d", [NP, 1])
        h_d = dram("h_d", [EP, 8])
        h2_d = dram("h2_d", [EP, 1])
        ex_d = dram("ex_d", [NC, P, 16])
        ex2_d = dram("ex2_d", [NC, P, 2])
        es_d = dram("es_d", [NC, CH], I32)
        ed_d = dram("ed_d", [NC, CH], I32)
        edp_d = dram("edp_d", [EP + 2], I32)
        ewt_d = dram("ewt_d", [NC, CH])
        trlo_d = dram("trlo_d", [J, P], BF16)
        ot_d = dram("ot_d", [P, J * P], BF16)
        hm_d = dram("hm_d", [P, J * NB], BF16)

        a0 = sb("a0", [P, 13000])
        a1 = sb("a1", [P, NB, D])
        xres = sb("xres", [P, NB, D])
        a3 = sb("a3", [P, 6400])
        src_n = sb("src_n", [P, J], I32)
        dst_n = sb("dst_n", [P, J], I32)
        w_n = a3[:, 1000:1000 + J]
        nh = sb("nh", [P, J])
        negh = sb("negh", [P, J])
        negt = sb("negt", [P, J])
        dl = sb("dl", [P, 2, 512])
        ndl = sb("ndl", [P, 2, 512])
        wsl = sb("wsl", [P, 2, 512])
        srci = sb("srci", [P, 2, 512], I32)
        br = sb("br", [4, P], I32)
        cr = sb("cr", [4, P], I32)
        w1s = sb("w1s", [P, 2, D])
        w2s = sb("w2s", [P, 2, D])
        wps = sb("wps", [P, 2, D])
        gw1s = sb("gw1s", [P, 2, 528])
        gw2s = sb("gw2s", [P, 4, 258])
        vec = sb("vec", [P, 7, D])
        att1 = sb("att1", [P, 2, 512])
        att2 = sb("att2", [P, 2, D])
        iota = sb("iota", [P, P])
        iotab = sb("iotab", [P, P], BF16)
        ident = sb("ident", [P, P])
        ones = sb("ones", [P, P])
        upper = sb("upper", [P, P])
        ioc = sb("ioc", [P, 32])
        sio = sb("sio", [P, 4])
        pidx = sb("pidx", [P, 1])
        small = sb("small", [P, 512])
        smalli = sb("smalli", [P, 64], I32)
        ends = sb("ends", [1, 2], I32)
        oh = sb("oh", [P, 4, 2, P])
        oht = sb("oht", [P, 2, P])
        exb = sb("exb", [P, 8, 16])
        yt = sb("yt", [P, 2, 512])
        stat = sb("stat", [P, NB, 6])
        mv = sb("mv", [P, NB, 2])
        rstd = sb("rstd", [P, NB])
        nmr = sb("nmr", [P, NB])
        elr = sb("elr", [P, NB, 16])
        den = sb("den", [P, NB, 8])
        sidx = sb("sidx", [P, NB], I32)
        deg = sb("deg", [P, NB])
        acol = sb("acol", [P, 4])
        ct = sb("ct", [8, 2, P + 1])
        cin = sb("cin", [P, 8])

        ps = psum("ps", [P, 8 * 512])
        pbig = [ps[:, 1024 * i:1024 * (i + 1)] for i in range(3)]
        tp = [ps[:, 512 * i:512 * (i + 1)] for i in (4, 5)]
        mp = [ps[:, 512 * i:512 * (i + 1)] for i in (6, 7)]

        def bc(ap, shape):
            return ap.to_broadcast(shape)

        c_i = G.do(lambda e: e.iota(iota[:, :], [[1, P]], base=0, channel_multiplier=0, allow_small_or_imprecise_dtypes=True))
        c_ib = G.do(lambda e: e.iota(iotab[:, :], [[1, P]], base=0, channel_multiplier=0, allow_small_or_imprecise_dtypes=True))
        c_ic = G.do(lambda e: e.iota(ioc[:, :], [[1, 32]], base=0, channel_multiplier=0, allow_small_or_imprecise_dtypes=True))
        c_s = G.do(lambda e: e.iota(sio[:, :], [[P, 4]], base=0, channel_multiplier=1, allow_small_or_imprecise_dtypes=True))
        c_pi = G.do(lambda e: e.iota(pidx[:, :], [[1, 1]], base=0, channel_multiplier=1, allow_small_or_imprecise_dtypes=True))
        c_z = G.do(lambda e: e.memset(ident[:, :], 0.0))
        c_id = G.do(lambda e: e.affine_select(out=ident[:, :], in_=ident[:, :], compare_op=ALU.not_equal, fill=1.0, base=0,
                                              pattern=[[-1, P]], channel_multiplier=1), c_z)
        c_on = G.do(lambda e: e.memset(ones[:, :], 1.0))
        c_zu = G.do(lambda e: e.memset(upper[:, :], 0.0))
        c_up = G.do(lambda e: e.affine_select(out=upper[:, :], in_=upper[:, :], compare_op=ALU.is_ge, fill=1.0, base=0,
                                              pattern=[[-1, P]], channel_multiplier=1), c_zu)
        ce = G.do(lambda e: e.memset(ends[:, 0:1], -1))
        ce = G.do(lambda e: e.memset(ends[:, 1:2], 5000), ce)

        m1 = V.do(lambda e: e.memset(dst_n[:, :], 4000))
        m2 = V.do(lambda e: e.memset(src_n[:, :], 0))
        m3 = V.do(lambda e: e.memset(w_n, 0.0))
        m4 = V.do(lambda e: e.memset(xres[:, NB - 1, :], 0.0))

        def nat(t, d, name, dep):
            lt = None
            for lo, p0, pn in ((0, 0, P - 1), (EFULL, P - 1, 1)):
                n = J if pn > 1 else E - EFULL
                lt = land(name).go(S, lambda e, lo=lo, p0=p0, pn=pn, n=n: e.dma_start(
                    t[p0:p0 + pn, 0:n], d[lo:lo + pn * n].rearrange("(p n) -> p n", n=n)), dep)
            return lt

        d_dst = nat(dst_n, dst, "dst", m1)
        half = 12
        d_x = land("x").go(S, lambda e: e.dma_start(xres[:, 0:half, :], x[0:half * P, :].rearrange("(b p) n -> p b n", p=P)))
        d_src = nat(src_n, src, "src", m2)
        d_w = nat(w_n, ew, "w", m3)
        land("x").go(S, lambda e: e.dma_start(xres[:, half:NB - 1, :], x[half * P:(NB - 1) * P, :].rearrange("(b p) n -> p b n", p=P)))
        d_x = land("x").go(S, lambda e: e.dma_start(xres[0:LAST, NB - 1, :], x[(NB - 1) * P:N, :]), m4)
        d_ed = land("ed").go(S, lambda e: e.dma_start(ed_d.rearrange("c k -> (c k)").rearrange("(p n) -> p n", n=J), dst_n[:, :]), d_dst)
        d_es = land("es").go(S, lambda e: e.dma_start(es_d.rearrange("c k -> (c k)").rearrange("(p n) -> p n", n=J), src_n[:, :]), d_src)
        d_ew = land("ewt").go(S, lambda e: e.dma_start(ewt_d.rearrange("c k -> (c k)").rearrange("(p n) -> p n", n=J), w_n), d_w)
        land("edp").go(S, lambda e: e.dma_start(edp_d[1:EP + 1].rearrange("(p n) -> p n", n=J), dst_n[:, :]), d_dst)
        land("edp").go(S, lambda e: e.dma_start(edp_d[0:1].rearrange("(p n) -> p n", n=1), ends[:, 0:1]), ce)
        d_edp = land("edp").go(S, lambda e: e.dma_start(edp_d[EP + 1:EP + 2].rearrange("(p n) -> p n", n=1), ends[:, 1:2]), ce)
        for t, d in ((w1s, w1), (w2s, w2), (wps, wp)):
            d_wt = land("wt").go(S, lambda e, t=t, d=d: e.dma_start(t[:, :, :], d.rearrange("(k p) n -> p k n", p=P)))
        land("wt").go(S, lambda e: e.dma_start(gw1s[:, :, 0:512], gw1.rearrange("(k p) n -> p k n", p=P)))
        land("wt").go(S, lambda e: e.dma_start(gw2s[:, :, 0:D], gw2.rearrange("(k p) n -> p k n", p=P)))
        for i, d in enumerate((b1, g1, be1, b2, g2, be2, bp)):
            land("wt").go(S, lambda e, i=i, d=d: e.dma_start(vec[:, i, :], d.rearrange("(o n) -> o n", o=1).to_broadcast([P, D])))
        for i, d in enumerate((al1, ar1)):
            land("wt").go(S, lambda e, i=i, d=d: e.dma_start(
                att1[:, i, :], d.rearrange("h d -> (h d)").rearrange("(o n) -> o n", o=1).to_broadcast([P, 512])))
        for i, d in enumerate((al2, ar2)):
            d_wt = land("wt").go(S, lambda e, i=i, d=d: e.dma_start(att2[:, i, :], d.to_broadcast([P, D])))

        cnt = small[:, 0:NB]
        junk = a3[:, 0:J]
        c0 = V.do(lambda e: e.memset(cnt, 0.0))
        for b in range(1, NB):
            c0 = V.do(lambda e, b=b: e.tensor_scalar(junk, dst_n[:, :], float(P * b), None, ALU.is_lt, ALU.add,
                                                     accum_out=small[:, b:b + 1]), d_dst, c0)
        eb = T.do(lambda e: e.matmul(tp[0][:, 0:NB], ones[:, :], cnt, start=True, stop=True), c0, c_on)
        v = V.do(lambda e: e.tensor_copy(smalli[:, 0:NB], tp[0][:, 0:NB]), eb)
        v = V.do(lambda e: e.tensor_scalar(smalli[:, 32:32 + NB], smalli[:, 0:NB], 8, None, ALU.arith_shift_right), v)
        v = V.do(lambda e: e.tensor_copy(small[:, 32:32 + NB], smalli[:, 32:32 + NB]), v)
        v = V.do(lambda e: e.tensor_tensor(small[:, 64:64 + NB], small[:, 32:32 + NB], ioc[:, 0:NB], ALU.add), v, c_ic)
        cmp = small[:, 128:128 + 96].rearrange("p (k b) -> p k b", k=4)
        v = V.do(lambda e: e.tensor_tensor(cmp, bc(sio[:, :].rearrange("p (k o) -> p k o", o=1), [P, 4, 24]),
                                           bc(small[:, 65:65 + 24].rearrange("p (o b) -> p o b", o=1), [P, 4, 24]),
                                           ALU.is_ge), v, c_s)
        bs = small[:, 256:260]
        cs = small[:, 260:264]
        nbs = small[:, 264:268]
        v = V.do(lambda e: e.tensor_reduce(bs, cmp, AX, ALU.add), v)
        V.do(lambda e: e.tensor_scalar(nbs, bs, -128.0, None, ALU.mult), v)
        v = V.do(lambda e: e.tensor_tensor(cs, sio[:, :], bs, ALU.subtract), v)
        v = V.do(lambda e: e.tensor_scalar(cs, cs, float(NC - 1), None, ALU.min), v)
        v_ci = V.do(lambda e: e.tensor_copy(smalli[:, 60:64], cs), v)
        rows = {}
        for i, (name, d, dep) in enumerate((("rs", es_d, d_es), ("rd", ed_d, d_ed), ("rw", ewt_d, d_ew))):
            o = a0[:, 1024 * i:1024 * (i + 1)]
            o = o.bitcast(I32) if i < 2 else o
            for k in range(4):
                rows[name] = land(name).go(G, lambda e, o=o, k=k, d=d: e.indirect_dma_start(
                    out=o[:, CH * k:CH * (k + 1)], out_offset=None, in_=d,
                    in_offset=bass.IndirectOffsetOnAxis(ap=smalli[:, 60 + k:61 + k], axis=0)), dep, v_ci)
        rsf = a0[:, 3072:4096]
        rdf = a0[:, 4096:5120]
        v_rs = V.do(lambda e: e.tensor_copy(rsf, a0[:, 0:1024].bitcast(I32)), rows["rs"])
        v_rd = None
        for k in range(4):
            v_rd = V.do(lambda e, k=k: e.tensor_scalar(rdf[:, CH * k:CH * (k + 1)], a0[:, 1024 + CH * k:1024 + CH * (k + 1)].bitcast(I32),
                                                       small[:, 264 + k:265 + k], None, ALU.add), rows["rd"], v)
        w = [None, None, None, None]
        n = 0
        banks = tp + mp
        tabs = []
        for f, dep, tab in ((rsf, v_rs, srci), (rdf, v_rd, dl), (a0[:, 2048:3072], rows["rw"], wsl)):
            for j in range(2):
                bk = banks[n % 4]
                for k in range(4):
                    t = T.do(lambda e, f=f, j=j, k=k, bk=bk: e.transpose(
                        bk[:, P * k:P * (k + 1)], f[:, CH * k + j:CH * (k + 1):2], ident[:, :]), dep, c_id, w[n % 4], v)
                w[n % 4] = V.do(lambda e, tab=tab, j=j, bk=bk: e.tensor_copy(tab[:, j, :], bk[:, :]), t)
                tabs.append(w[n % 4])
                n += 1
        v_tab = tabs[-1]
        v_ndl = V.do(lambda e: e.tensor_scalar(ndl[:, :, :], dl[:, :, :], -1.0, None, ALU.mult), v_tab)
        for i, (q, tab) in enumerate(((bs, br), (cs, cr))):
            t = T.do(lambda e, q=q, i=i: e.transpose(banks[i][0:4, 0:P], q, ident[:, :]), v_tab)
            v_reg = V.do(lambda e, i=i, tab=tab: e.tensor_copy(tab[:, :], banks[i][0:4, 0:P]), t)

        def stats(b, ap, *deps):
            s = V.do(lambda e: e.bn_stats(stat[:, b, :], ap), *deps)
            return V.do(lambda e: e.bn_aggr(mv[:, b, :], stat[:, b, :]), s)

        def scales(dep):
            s = V.do(lambda e: e.tensor_scalar(nmr[:, :], mv[:, :, 1], EPS, None, ALU.add), dep)
            s = A.do(lambda e: e.activation(rstd[:, :], nmr[:, :], ACT.Sqrt), s)
            s = V.do(lambda e: e.reciprocal(rstd[:, :], rstd[:, :]), s)
            s = V.do(lambda e: e.tensor_tensor(nmr[:, :], mv[:, :, 0], rstd[:, :], ALU.mult), s)
            return V.do(lambda e: e.tensor_scalar(nmr[:, :], nmr[:, :], -1.0, None, ALU.mult), s)

        def norm(b, o, i, func, *deps):
            return A.do(lambda e: e.activation(o, i, func, bias=nmr[:, b:b + 1], scale=rstd[:, b:b + 1]), *deps)

        GRP = 5

        def store(t, name, b, tok):
            if b % GRP == GRP - 1:
                return land(name).go(S, lambda e: e.dma_start(
                    t[(b - GRP + 1) * P:(b + 1) * P, :].rearrange("(b p) n -> p b n", p=P), a1[:, b - GRP + 1:b + 1, :]), tok)
            return None

        for b in range(NB):
            v = stats(b, xres[:, b, :], d_x)
        v = scales(v)
        for b in range(NB):
            a = norm(b, a1[:, b, :], xres[:, b, :], ACT.Relu, v)
            store(t0, "t0", b, a)

        NR = 6
        ring_free = [None] * 8
        oh_free = [None] * 4
        ps_free = [None] * 3
        ex_free = [None] * 8
        regs = {}

        def block_of(e, s):
            if s % 4 == 0:
                if "b" not in regs:
                    regs["b"] = [e.alloc_register(f"rb{i}") for i in range(4)]
                k = s // P
                e.load(regs["b"], br[k:k + 1, s % P:s % P + 4])
            return e.snap(regs["b"][s % 4], min_val=0, max_val=NB - 1)

        def chunk_of(e, s):
            if s % 4 == 0:
                if "c" not in regs:
                    regs["c"] = [e.alloc_register(f"rc{i}") for i in range(4)]
                k = s // P
                e.load(regs["c"], cr[k:k + 1, s % P:s % P + 4])
            return e.snap(regs["c"][s % 4], min_val=0, max_val=NC - 1)

        def aggregate(name, table, mode, acc, start, side=None):
            F = 512 if mode == "heads" else 256
            W = {"weights": 256, "heads": 520, "one": 257}[mode]
            nr = NR
            exd = {"heads": ex_d, "one": ex2_d}.get(mode)
            ew_ = 16 if mode == "heads" else 2
            pend = []
            done = start
            for s in range(NS):
                r = s % nr
                buf = [a3[:, (2 * r + k) * 512:(2 * r + k) * 512 + F] for k in range(2)]
                if exd is not None:
                    q = s % 8
                    x_in = land(f"ex{q}").go(S, lambda e, s=s, q=q: e.dma_start(
                        exb[:, q, 0:ew_], exd[bass.ds(chunk_of(e, s), 1), :, :].rearrange("o p f -> (o p) f")), ex_free[q], start, v_reg)
                for k in range(2):
                    g_in = land(f"g{r}").go(G, lambda e, s=s, k=k, buf=buf: e.indirect_dma_start(
                        out=buf[k], out_offset=None, in_=table,
                        in_offset=bass.IndirectOffsetOnAxis(ap=srci[:, k, s:s + 1], axis=0)), ring_free[r], start, v_tab)
                so = s % 4
                oks = []
                for k in range(2):
                    o = oh[:, so, k, :]
                    if mode == "heads":
                        a = A.do(lambda e, s=s, k=k: e.activation(oht[:, k, :], iota[:, :], ACT.Abs, bias=ndl[:, k, s:s + 1]),
                                 v_ndl, c_i, oh_free[so])
                        ok = A.do(lambda e, k=k, o=o: e.activation(o, oht[:, k, :], ACT.Relu, bias=1.0, scale=-1.0), a)
                    else:
                        sc = wsl[:, k, s:s + 1] if mode == "weights" else exb[:, s % 8, k:k + 1]
                        ok = V.do(lambda e, s=s, k=k, o=o, sc=sc: e.tensor_scalar(o, iota[:, :], dl[:, k, s:s + 1], sc, ALU.is_equal, ALU.mult),
                                  v_tab, c_i, oh_free[so], x_in if exd is not None else None)
                    oks.append(ok)
                if mode == "heads":
                    for k in range(2):
                        bv = buf[k].rearrange("p (h d) -> p h d", h=8)
                        mk = V.do(lambda e, k=k, bv=bv, s=s: e.tensor_tensor(
                            bv, bv, bc(exb[:, s % 8, 8 * k:8 * k + 8].rearrange("p (h o) -> p h o", o=1), [P, 8, 64]), ALU.mult), g_in, x_in)
                        oks.append(mk)
                if len(pend) == 2:
                    done = pend.pop(0)()
                pp = pbig[s % 3]
                t = None
                for k in range(2):
                    t = T.do(lambda e, pp=pp, so=so, k=k, buf=buf: e.matmul(pp[:, 0:F], oh[:, so, k, :], buf[k], start=(k == 0), stop=(k == 1)),
                             *oks, g_in, ps_free[s % 3])
                if mode != "weights":
                    for k in range(2):
                        rhs = exb[:, s % 8, 8 * k:8 * k + 8] if mode == "heads" else ones[:, 0:1]
                        off = 512 if mode == "heads" else 256
                        t = T.do(lambda e, pp=pp, so=so, k=k, rhs=rhs, off=off: e.matmul(
                            pp[:, 512:512 + W - off], oh[:, so, k, :], rhs, start=(k == 0), stop=(k == 1)), x_in)
                ring_free[r] = t
                oh_free[so] = t
                if exd is not None:
                    ex_free[s % 8] = t

                def evac(s=s, t=t, pp=pp):
                    def add(e):
                        b = block_of(e, s)
                        d = acc[:, bass.ds(b * W, W)]
                        if mode == "one":
                            d = acc[:, bass.ds(b * W, 256)]
                            return e.tensor_tensor(d, d, pp[:, 0:256], ALU.add)
                        return e.tensor_tensor(d, d, pp[:, 0:W], ALU.add)
                    tok = V.do(add, t, done, v_reg)
                    if mode == "one":
                        def add2(e):
                            b = e.snap(regs["b"][s % 4], min_val=0, max_val=NB - 1)
                            d = acc[:, bass.ds(b * W + 256, 1)]
                            return e.tensor_tensor(d, d, pp[:, 512:513], ALU.add)
                        tok = V.do(add2)
                    ps_free[s % 3] = tok
                    return tok
                pend.append(evac)
                if side is not None:
                    side(s)
            for f in pend:
                done = f()
            return done

        dn = [0]
        tfree, mfree, yfree = [None, None], [None, None], [None, None]

        def dense(inp, K, ws, Nc, dep, extra=0):
            i = dn[0] % 2
            dn[0] += 1
            for k in range(K):
                t = T.do(lambda e, k=k: e.transpose(tp[i][:, P * k:P * (k + 1)], inp[:, P * k:P * (k + 1)], ident[:, :]),
                         dep, c_id, tfree[i])
            c = A.do(lambda e: e.activation(yt[:, i, 0:P * K], tp[i][:, 0:P * K], ACT.Copy), t, yfree[i])
            tfree[i] = c
            for k in range(K):
                t = T.do(lambda e, k=k: e.matmul(mp[i][:, 0:Nc], yt[:, i, P * k:P * (k + 1)], ws[:, k, 0:Nc],
                                                 start=(k == 0), stop=(k == K - 1)), c, d_wt, mfree[i])
            if extra:
                for k in range(K):
                    t = T.do(lambda e, k=k: e.matmul(pbig[i][:, 0:extra], yt[:, i, P * k:P * (k + 1)], ws[:, k, Nc:Nc + extra],
                                                     start=(k == 0), stop=(k == K - 1)))
            yfree[i] = t
            return i, t

        a1f = a1[:, :, :].rearrange("p b n -> p (b n)")
        hb = a0[:, 6400:12800].rearrange("p (b n) -> p b n", n=D)

        lo = a0[:, 0:J]
        hi = a0[:, 800:800 + J]
        dti = a0[:, 1600:1600 + J].bitcast(I32)
        ohl = a0[:, 2400:2400 + 2 * 1024].bitcast(BF16).rearrange("p (u j d) -> p u j d", u=2, j=16)
        ohh = a0[:, 5000:5000 + 2 * 256].bitcast(BF16).rearrange("p (u j d) -> p u j d", u=2, j=16)
        hst = {"free": [None, None], "t": None}

        def bits():
            v = V.do(lambda e: e.tensor_scalar(dti, dst_n[:, :], 127, None, ALU.bitwise_and), v_reg)
            v = V.do(lambda e: e.tensor_copy(lo, dti), v)
            v = V.do(lambda e: e.tensor_scalar(dti, dst_n[:, :], 7, None, ALU.arith_shift_right), v)
            hst["v"] = V.do(lambda e: e.tensor_copy(hi, dti), v)

        def histogram(s):
            if s % 8 != 4 or s // 8 >= 49:
                return
            g = s // 8
            j0, jn = 16 * g, min(16, J - 16 * g)
            u = g % 2
            v1 = V.do(lambda e: e.tensor_tensor(ohl[:, u, 0:jn, :], bc(iotab[:, :].rearrange("p (o d) -> p o d", o=1), [P, jn, P]),
                                                bc(lo[:, j0:j0 + jn].rearrange("p (j o) -> p j o", o=1), [P, jn, P]), ALU.is_equal),
                      c_ib, hst["v"], hst["free"][u])
            v2 = V.do(lambda e: e.tensor_tensor(ohh[:, u, 0:jn, 0:NB], bc(iotab[:, 0:NB].rearrange("p (o d) -> p o d", o=1), [P, jn, NB]),
                                                bc(hi[:, j0:j0 + jn].rearrange("p (j o) -> p j o", o=1), [P, jn, NB]), ALU.is_equal))
            for i in range(jn):
                t = T.do(lambda e, i=i: e.matmul(mp[0][:, 0:NB], ohl[:, u, i, :], ohh[:, u, i, 0:NB],
                                                 start=(j0 + i == 0), stop=(j0 + i == J - 1)), v2)
            hst["free"][u] = hst["t"] = t

        bits()
        d_t0 = land("t0").sem, land("t0").n
        tok = aggregate("l0", t0, "weights", a1f, d_t0, histogram)

        v = V.do(lambda e: e.tensor_copy(deg[:, :], mp[0][:, 0:NB]), hst["t"])
        t = T.do(lambda e: e.matmul(tp[0][:, 0:NB], ones[:, :], deg[:, :], start=True, stop=True), v)
        t = T.do(lambda e: e.matmul(tp[1][:, 0:NB], upper[:, :], deg[:, :], start=True, stop=True), c_up)
        v = V.do(lambda e: e.tensor_copy(small[:, 0:NB], tp[0][:, 0:NB]), t)
        v = V.do(lambda e: e.tensor_tensor_scan(small[:, 32:32 + NB], ones[:, 0:NB], small[:, 0:NB], 0.0, ALU.mult, ALU.add), v)
        v = V.do(lambda e: e.tensor_tensor(small[:, 64:64 + NB], small[:, 32:32 + NB], small[:, 0:NB], ALU.subtract), v)
        v = V.do(lambda e: e.tensor_tensor(small[:, 64:64 + NB], small[:, 64:64 + NB], tp[1][:, 0:NB], ALU.add), v)
        v = V.do(lambda e: e.tensor_scalar(small[:, 96:96 + NB], deg[:, :], 0.0, 1.0e6, ALU.is_equal, ALU.mult), v)
        v = V.do(lambda e: e.tensor_tensor(small[:, 64:64 + NB], small[:, 64:64 + NB], small[:, 96:96 + NB], ALU.add), v)
        v_sidx = V.do(lambda e: e.tensor_copy(sidx[:, :], small[:, 64:64 + NB]), v)
        tfree[0] = tfree[1] = mfree[0] = v_sidx

        def conv_dense(tok, ws, ib, last):
            for b in range(NB):
                i, t = dense(a1[:, b, :], 2, ws, D, tok)
                v = V.do(lambda e, i=i, b=b: e.tensor_tensor(hb[:, b, :], mp[i][:, 0:D], vec[:, ib, :], ALU.add), t)
                mfree[i] = v
                v = stats(b, hb[:, b, :], v)
            v = scales(v)
            toks = []
            for b in range(NB):
                a = norm(b, hb[:, b, :], hb[:, b, :], ACT.Identity, v)
                g = V.do(lambda e, b=b: e.tensor_tensor(hb[:, b, :], hb[:, b, :], vec[:, ib + 1, :], ALU.mult), a)
                toks.append(V.do(lambda e, b=b: e.tensor_tensor(hb[:, b, :], hb[:, b, :], vec[:, ib + 2, :], ALU.add), g))
            outs = []
            for b in range(NB):
                outs.append(A.do(lambda e, b=b: e.activation(a1[:, b, :], hb[:, b, :], ACT.Gelu), toks[b]))
                if last is not None:
                    store(last, "t1", b, outs[-1])
            return outs

        conv_dense(tok, w1s, 0, t1)
        d_t1 = land("t1").sem, land("t1").n

        dpn = a0[:, 0:J].bitcast(I32)
        dnn = a0[:, 800:800 + J].bitcast(I32)

        def flags():
            land("dp").go(S, lambda e: e.dma_start(dpn, edp_d[0:EP].rearrange("(p n) -> p n", n=J)), d_edp, tok)
            l = land("dp").go(S, lambda e: e.dma_start(dnn, edp_d[2:EP + 2].rearrange("(p n) -> p n", n=J)), d_edp, tok)
            V.do(lambda e: e.tensor_tensor(nh[:, :], dst_n[:, :], dpn, ALU.is_equal), l)
            v = V.do(lambda e: e.tensor_tensor(negt[:, :], dst_n[:, :], dnn, ALU.is_equal))
            V.do(lambda e: e.tensor_scalar(negh[:, :], nh[:, :], BIG, -BIG, ALU.mult, ALU.add), v)
            v = V.do(lambda e: e.tensor_scalar(negt[:, :], negt[:, :], BIG, -BIG, ALU.mult, ALU.add), v)
            for i, q in enumerate((nh, negh, negt)):
                v2 = V.do(lambda e, i=i, q=q: e.tensor_reduce(acol[:, i:i + 1], q[:, :], AX, ALU.min), v)
            return v2

        v_fl = flags()
        z = V.do(lambda e: e.memset(a3[:, :], 0.0), tok)
        land("hz").go(S, lambda e: e.dma_start(h_d.rearrange("e h -> (e h)").rearrange("(p n) -> p n", p=P), a3[:, 0:J * 8]), z)
        d_hz = land("hz").go(S, lambda e: e.dma_start(h2_d.rearrange("e h -> (e h)").rearrange("(p n) -> p n", p=P), a3[:, 0:J]), z)
        ring_free[0:NR] = [d_hz] * NR

        f = v_fl
        for k in range(2):
            for i in range(2):
                f = V.do(lambda e, k=k, i=i: e.tensor_tensor(a0[:, 2000:2512], gw1s[:, k, 0:512], att1[:, i, :], ALU.mult), d_wt, f)
                f = V.do(lambda e, k=k, i=i: e.tensor_reduce(gw1s[:, k, 512 + 8 * i:520 + 8 * i],
                                                             a0[:, 2000:2512].rearrange("p (h d) -> p h d", h=8), AX, ALU.add), f)
        for k in range(4):
            for i in range(2):
                f = V.do(lambda e, k=k, i=i: e.tensor_tensor(a0[:, 2000:2256], gw2s[:, k, 0:D], att2[:, i, :], ALU.mult), f)
                f = V.do(lambda e, k=k, i=i: e.tensor_reduce(gw2s[:, k, D + i:D + i + 1], a0[:, 2000:2256], AX, ALU.add), f)
        v_fold = f

        slo = a0[:, 4000:4000 + J]
        shi = a0[:, 4800:4800 + J]
        sti = a0[:, 5600:5600 + J].bitcast(I32)
        trb = a0[:, 2600:2600 + 448].bitcast(BF16).rearrange("p (g e) -> p g e", e=P)
        v = V.do(lambda e: e.tensor_scalar(sti, src_n[:, :], 127, None, ALU.bitwise_and), v_fold)
        v = V.do(lambda e: e.tensor_copy(slo, sti), v)
        v = V.do(lambda e: e.tensor_scalar(sti, src_n[:, :], 7, None, ALU.arith_shift_right), v)
        v_shi = V.do(lambda e: e.tensor_copy(shi, sti), v)
        v = v_shi
        for g in range(7):
            n = min(P, J - P * g)
            t = T.do(lambda e, g=g, n=n: e.transpose(tp[g // 4][0:n, P * (g % 4):P * (g % 4 + 1)], slo[:, P * g:P * g + n], ident[:, :]), v)
        for g in range(7):
            n = min(P, J - P * g)
            v = V.do(lambda e, g=g, n=n: e.tensor_copy(trb[0:n, g, :], tp[g // 4][0:n, P * (g % 4):P * (g % 4 + 1)]), t)
        d_tr = land("tr").go(S, lambda e: e.dma_start(trlo_d[0:6 * P, :].rearrange("(g j) e -> j g e", j=P), trb[:, 0:6, :]), v)
        d_tr = land("tr").go(S, lambda e: e.dma_start(trlo_d[6 * P:J, :], trb[0:J - 6 * P, 6, :]), v)
        tfree[0] = tfree[1] = ps_free[2] = v
        obb = a0[:, 6400:8448].bitcast(BF16).rearrange("p (u n) -> p u n", u=2)
        obo = a0[:, 8448:10496].bitcast(BF16).rearrange("p (u n) -> p u n", u=2)
        obh = a0[:, 10496:10896].bitcast(BF16).rearrange("p (u j d) -> p u j d", u=2, d=NB)
        otf = {"b": [None, None], "o": [None, None]}

        def one_hots(s):
            if s % 8 != 4 or s // 8 >= NG:
                return
            g = s // 8
            jn = min(16, J - 16 * g)
            u = g % 2
            l = land(f"ob{u}").go(S, lambda e: e.dma_start(obb[:, u, 0:jn * P], trlo_d[16 * g:16 * g + jn, :].rearrange("j e -> (j e)").rearrange(
                "(o n) -> o n", o=1).to_broadcast([P, jn * P])), d_tr, otf["b"][u])
            v = V.do(lambda e: e.tensor_scalar(obo[:, u, 0:jn * P], obb[:, u, 0:jn * P], pidx[:, :], None, ALU.is_equal), l, c_pi, otf["o"][u])
            otf["b"][u] = v
            v = V.do(lambda e: e.tensor_tensor(obh[:, u, 0:jn, :], bc(iotab[:, 0:NB].rearrange("p (o d) -> p o d", o=1), [P, jn, NB]),
                                               bc(shi[:, 16 * g:16 * g + jn].rearrange("p (j o) -> p j o", o=1), [P, jn, NB]), ALU.is_equal), v_shi)
            land(f"oo{u}").go(S, lambda e: e.dma_start(ot_d[:, 2048 * g:2048 * g + jn * P], obo[:, u, 0:jn * P]), v)
            otf["o"][u] = land(f"oo{u}").go(S, lambda e: e.dma_start(hm_d[:, 400 * g:400 * g + jn * NB], obh[:, u, 0:jn, :].rearrange("p j d -> p (j d)")), v)

        tok = aggregate("l1", t1, "weights", a1f, d_t1, one_hots)
        S.need(*otf["o"])
        V.need(*otf["o"])
        A.need(*otf["o"])
        outs = conv_dense(tok, w2s, 3, None)
        for b in range(NB):
            i, t = dense(a1[:, b, :], 2, wps, D, outs[b])
            v = V.do(lambda e, i=i, b=b: e.tensor_tensor(hb[:, b, :], mp[i][:, 0:D], vec[:, 6, :], ALU.add), t)
            mfree[i] = v
            v = V.do(lambda e, b=b: e.tensor_tensor(xres[:, b, :], xres[:, b, :], hb[:, b, :], ALU.add), v)
            v = stats(b, xres[:, b, :], v)
        v = scales(v)
        stage = a3[:, 0:2048].rearrange("p (u n) -> p u n", n=512)
        sfree = [None] * 4
        for b in range(NB):
            a = norm(b, a1[:, b, :], xres[:, b, :], ACT.Relu, v)
            i, t = dense(a1[:, b, :], 2, gw1s, 512, a, 16)
            T.need(v_fold)
            u = b % 4
            c = V.do(lambda e, i=i, u=u: e.tensor_copy(stage[:, u, :], mp[i][:, :]), t, sfree[u])
            c = V.do(lambda e, i=i, b=b: e.tensor_copy(elr[:, b, :], pbig[i][:, 0:16]))
            mfree[i] = c
            sfree[u] = land(f"st{u}").go(S, lambda e, b=b, u=u: e.dma_start(t2[b * P:(b + 1) * P, :], stage[:, u, :]), c)
        d_el = land("el").go(S, lambda e: e.dma_start(el_d.rearrange("(b p) h -> p b h", p=P), elr[:, :, 0:8]), c)
        t2_ready = list(sfree)
        for u in range(4):
            ring_free[u] = sfree[u]
        V.need(*sfree)
        S.need(*sfree)
        t2_land = c

        def carry(lcol, acolumn, H, op0, op1, init, back, dep):
            t = T.do(lambda e: e.transpose(tp[0][0:H, 0:P], lcol, ident[:, :]), dep)
            t = T.do(lambda e: e.transpose(tp[1][0:H, 0:P], bc(acolumn, [P, H]), ident[:, :]), v_fl)
            v = V.do(lambda e: e.tensor_copy(ct[0:H, 0, 0:P], tp[1][0:H, 0:P]), t)
            v = V.do(lambda e: e.memset(ct[0:H, 1, :], init), v)
            if not back:
                v = V.do(lambda e: e.tensor_tensor_scan(ct[0:H, 1, 1:P + 1], ct[0:H, 0, 0:P], tp[0][0:H, 0:P], init, op0, op1), v)
                c = ct[0:H, 1, 0:P]
            else:
                v = V.do(lambda e: e.tensor_tensor_scan(ct[0:H, 1, 0:P][:, ::-1], ct[0:H, 0, 0:P][:, ::-1],
                                                        tp[0][0:H, 0:P][:, ::-1], init, op0, op1), v)
                c = ct[0:H, 1, 1:P + 1]
            t = T.do(lambda e: e.transpose(tp[0][:, 256:256 + H], c, ident[0:H, 0:H]), v)
            return V.do(lambda e: e.tensor_copy(cin[:, 0:H], tp[0][:, 256:256 + H]), t)

        def scan(H, o, i, f, ac, op0, op1, init, back, dep):
            st = -1 if back else 1
            v = dep
            for first in (True, False):
                for h in range(H):
                    ini = init if first else cin[:, h:h + 1]
                    vv = V.do(lambda e, h=h, ini=ini: e.tensor_tensor_scan(
                        o[:, :, h][:, ::st], f[:, ::st], i[:, :, h][:, ::st], ini, op0, op1), v)
                v = vv
                if first:
                    edge = 0 if back else J - 1
                    v = carry(o[:, edge, :], ac, H, op0, op1, init, back, v)
            return v

        tbl = sb("tbl", [P, 3, 200], BF16)

        def lookup(H, elv, el_sb, groups, dep):
            el = el_sb.rearrange("p b h -> p h b")
            W = H * NB
            tv = [tbl[:, i, 0:W].rearrange("p (h b) -> p h b", h=H) for i in range(3)]
            r = a1f[:, 0:W].rearrange("p (h b) -> p h b", h=H)
            v = V.do(lambda e: e.tensor_copy(tv[0], el), dep)
            v = V.do(lambda e: e.tensor_tensor(r, el, tv[0], ALU.subtract), v)
            v = V.do(lambda e: e.tensor_copy(tv[1], r), v)
            v = V.do(lambda e: e.tensor_tensor(r, r, tv[1], ALU.subtract), v)
            v_t = V.do(lambda e: e.tensor_copy(tv[2], r), v)
            NU = 4
            ot = a3[:, 0:1024 * NU].bitcast(BF16).rearrange("p (u n) -> p u n", u=NU)
            hm = a3[:, 1024 * NU:1224 * NU].bitcast(BF16).rearrange("p (u j d) -> p u j d", u=NU, d=NB)
            tmp = a1f[:, 400:400 + 1600].rearrange("p (u n) -> p u n", u=2)
            per, stride = (4, 256) if H == 8 else (16, 32)
            tf, of, pf = [v_t, v_t], [dep] * NU, [v_t] * 3
            cnt = [0]

            def part(g, u, q, m, l):
                b, c = cnt[0] % 3, cnt[0] % 2
                cnt[0] += 1
                pp = pbig[b][:, 0:per * stride].rearrange("p (t w) -> p t w", w=stride)
                for i in range(m):
                    for k in range(3):
                        t = T.do(lambda e, i=i, k=k: e.matmul(pp[:, i, 0:W], ot[:, u, (q + i) * P:(q + i + 1) * P], tbl[:, k, 0:W],
                                                              start=(k == 0), stop=(k == 2)), l, v_t, pf[b])
                tv4 = tmp[:, c, 0:m * W].rearrange("p (t h d) -> p t h d", t=m, d=NB)
                v = V.do(lambda e: e.tensor_tensor(tv4, pp[:, 0:m, 0:W].rearrange("p t (h d) -> p t h d", d=NB),
                                                   bc(hm[:, u, q:q + m, :].rearrange("p t (o d) -> p t o d", o=1), [P, m, H, NB]),
                                                   ALU.mult), t, l, tf[c])
                pf[b] = of[u] = v
                j0 = 16 * g + q
                tf[c] = V.do(lambda e: e.tensor_reduce(elv[:, j0:j0 + m, :].rearrange("p t h -> p (t h)"),
                                                       tmp[:, c, 0:m * W].rearrange("p (x d) -> p x d", d=NB), AX, ALU.add), v)

            def group(g):
                jn = min(16, J - 16 * g)
                u = g % NU
                land(f"ot{u}").go(S, lambda e: e.dma_start(ot[:, u, 0:jn * P], ot_d[:, 2048 * g:2048 * g + jn * P]), of[u])
                l = land(f"ot{u}").go(S, lambda e: e.dma_start(hm[:, u, 0:jn, :].rearrange("p j d -> p (j d)"), hm_d[:, 400 * g:400 * g + jn * NB]))
                for q in range(0, jn, per):
                    part(g, u, q, min(per, jn - q), l)

            for g in range(groups):
                group(g)
            return tf[0], tf[1]

        def attention(H, eld, elsem, el_sb, er_sb, hd, exd_flat, dep, groups, look):
            elv = a0[:, 0:J * H].rearrange("p (j h) -> p j h", h=H)
            erv = a0[:, 6400:6400 + J * H].rearrange("p (j h) -> p j h", h=H)
            fv = a1f[:, 0:J * H].rearrange("p (j h) -> p j h", h=H)
            mvv = a3[:, 0:J * H].rearrange("p (j h) -> p j h", h=H)
            flat = [q for q in (a0[:, 0:J * H], a0[:, 6400:6400 + J * H], a1f[:, 0:J * H], a3[:, 0:J * H])]
            for b in range(NB):
                d = land(f"sc{H}").go(G, lambda e, b=b: e.indirect_dma_start(
                    out=hd, out_offset=bass.IndirectOffsetOnAxis(ap=sidx[:, b:b + 1], axis=0), in_=er_sb(b), in_offset=None,
                    bounds_check=EP - 1, oob_is_err=False), dep, v_sidx, d_hz)
            l = land(f"hl{H}").go(S, lambda e: e.dma_start(flat[1], hd.rearrange("e h -> (e h)").rearrange("(p n) -> p n", p=P)), d)
            toks = lookup(H, elv, el_sb, groups, look)
            g = None
            for j in range(16 * groups, J):
                g = land(f"eg{H}").go(G, lambda e, j=j: e.indirect_dma_start(
                    out=elv[:, j, :], out_offset=None, in_=eld,
                    in_offset=bass.IndirectOffsetOnAxis(ap=src_n[:, j:j + 1], axis=0)), elsem)
            V.need(*toks, l)
            v = scan(H, mvv, erv, nh, acol[:, 0:1], ALU.mult, ALU.add, 0.0, False, toks[0])
            v = scan(H, fv, elv, negh, acol[:, 1:2], ALU.add, ALU.max, -BIG, False, (V.need(g), v)[1])
            v = scan(H, erv, fv, negt, acol[:, 2:3], ALU.add, ALU.max, -BIG, True, v)
            v = V.do(lambda e: e.tensor_tensor(flat[1], flat[1], flat[3], ALU.add), v)
            v = V.do(lambda e: e.scalar_tensor_tensor(out=flat[1], in0=flat[1], scalar=0.2, in1=flat[1], op0=ALU.mult, op1=ALU.max), v)
            v = V.do(lambda e: e.tensor_tensor(flat[0], flat[0], flat[3], ALU.add), v)
            v = V.do(lambda e: e.scalar_tensor_tensor(out=flat[0], in0=flat[0], scalar=0.2, in1=flat[0], op0=ALU.mult, op1=ALU.max), v)
            v = V.do(lambda e: e.tensor_tensor(flat[0], flat[0], flat[1], ALU.subtract), v)
            a = A.do(lambda e: e.activation(flat[2], flat[0], ACT.Exp), v)
            return land(f"exs{H}").go(S, lambda e: e.dma_start(exd_flat, flat[2]), a), a

        S.need(c)
        d_ex, a = attention(8, el_d, d_el, elr[:, :, 0:8], lambda b: elr[:, b, 8:16], h_d,
                            ex_d.rearrange("c p f -> (c p f)").rearrange("(p n) -> p n", p=P), c, 35, t2_land)
        acc1 = a0[:, :]
        z = V.do(lambda e: e.memset(acc1, 0.0), a)
        G.need(a, *t2_ready)
        ps_free[:] = [mfree[0], mfree[1], None]
        tok = aggregate("g1", t2, "heads", acc1, d_ex)
        a13 = acc1.rearrange("p (b w) -> p b w", w=520)
        v = V.do(lambda e: e.tensor_scalar(den[:, :, :], a13[:, :, 512:520], 1e-30, None, ALU.max), tok)
        v = V.do(lambda e: e.reciprocal(den[:, :, :], den[:, :, :]), v)
        etmp = a3[:, 0:4096].rearrange("p (u n) -> p u n", n=512)
        v0 = v
        for b in range(NB):
            u = 2 * (b % 4)
            blk = a13[:, b, 0:512].rearrange("p (h d) -> p h d", h=8)
            v = V.do(lambda e, b=b, blk=blk: e.tensor_tensor(blk, blk, bc(den[:, b, :].rearrange("p (h o) -> p h o", o=1), [P, 8, 64]), ALU.mult), v0)
            v = V.do(lambda e, b=b, u=u: e.tensor_scalar(etmp[:, u, :], a13[:, b, 0:512], 0.0, None, ALU.min), v)
            a = A.do(lambda e, u=u: e.activation(etmp[:, u + 1, :], etmp[:, u, :], ACT.Exp), v)
            v = V.do(lambda e, b=b: e.tensor_scalar(a13[:, b, 0:512], a13[:, b, 0:512], 0.0, -1.0, ALU.max, ALU.add), v)
            v = V.do(lambda e, b=b, u=u: e.tensor_tensor(a13[:, b, 0:512], a13[:, b, 0:512], etmp[:, u + 1, :], ALU.add), a, v)
            i, t = dense(a13[:, b, 0:512], 4, gw2s, D, v, 2)
            c = V.do(lambda e, i=i, b=b: e.tensor_copy(a1[:, b, :], mp[i][:, 0:D]), t)
            c = V.do(lambda e, i=i, b=b: e.tensor_copy(elr[:, b, 0:2], pbig[i][:, 0:2]))
            mfree[i] = c
            store(t3, "t3", b, c)
        d_t3 = land("t3").sem, land("t3").n
        d_el2 = land("el2").go(S, lambda e: e.dma_start(el2_d.rearrange("(b p) h -> p b h", p=P), elr[:, :, 0:1], allow_slow_non_contiguous=True), c)
        V.need(d_t3)
        G.need(c)
        d_ex2, a = attention(1, el2_d, d_el2, elr[:, :, 0:1], lambda b: elr[:, b, 1:2], h2_d,
                             ex2_d.rearrange("c p f -> (c p f)").rearrange("(p n) -> p n", p=P), c, NG, d_t3)
        acc2 = a0[:, 0:NB * 257]
        z = V.do(lambda e: e.memset(acc2, 0.0), a)
        G.need(a)
        ps_free[:] = [mfree[0], mfree[1], None]
        S.need(d_t3)
        G.need(d_t3)
        tok = aggregate("g2", t3, "one", acc2, d_ex2)
        a23 = acc2.rearrange("p (b w) -> p b w", w=257)
        v = V.do(lambda e: e.tensor_scalar(deg[:, :], a23[:, :, 256], 1e-30, None, ALU.max), tok)
        v = V.do(lambda e: e.reciprocal(deg[:, :], deg[:, :]), v)
        v0 = v
        for b in range(NB):
            v = V.do(lambda e, b=b: e.scalar_tensor_tensor(out=a1[:, b, :], in0=a23[:, b, 0:D], scalar=deg[:, b:b + 1], in1=xres[:, b, :],
                                                           op0=ALU.mult, op1=ALU.add), v0)
            if b < NB - 1 and b % 6 == 5:
                land("out").go(S, lambda e, b=b: e.dma_start(out[(b - 5) * P:(b + 1) * P, :].rearrange("(b p) n -> p b n", p=P),
                                                             a1[:, b - 5:b + 1, :]), v)
        fin = land("out").go(S, lambda e: e.dma_start(out[(NB - 1) * P:N, :], a1[0:LAST, NB - 1, :]), v)
        S.need(fin)

        block = ctx.enter_context(nc.Block())

        @block.sync
        def _(e):
            S.replay(e)

        @block.gpsimd
        def _(e):
            G.replay(e)

        @block.scalar
        def _(e):
            A.replay(e)

        @block.vector
        def _(e):
            V.replay(e)

        @block.tensor
        def _(e):
            T.replay(e)


_INS = ["x", "src", "dst", "edge_weight", "L0_gnn_W1", "L0_gnn_b1", "L0_gnn_g1", "L0_gnn_be1", "L0_gnn_W2", "L0_gnn_b2",
        "L0_gnn_g2", "L0_gnn_be2", "L0_gnn_Wp", "L0_gnn_bp", "L1_gnn_W1", "L1_gnn_attn_l1", "L1_gnn_attn_r1", "L1_gnn_W2",
        "L1_gnn_attn_l2", "L1_gnn_attn_r2"]
_OUTS = [((N, D), "float32")]


def kernel(**inputs):
    import numpy as _np
    import concourse.bacc as _bacc
    from concourse import mybir as _mybir
    from concourse.bass_utils import run_bass_kernel_spmd as _run

    nc = _bacc.Bacc("TRN2", target_bir_lowering=False, num_devices=1)
    arrays, args = {}, []
    for name in _INS:
        a = _np.ascontiguousarray(inputs[name])
        arrays[f"in_{name}_dram"] = a
        args.append(nc.dram_tensor(f"in_{name}_dram", a.shape, _mybir.dt.from_np(a.dtype), kind="ExternalInput").ap())
    for i, (shape, dtype) in enumerate(_OUTS):
        dt = _mybir.dt.from_np(_np.dtype(dtype))
        args.append(nc.dram_tensor(f"out_{i}_dram", shape, dt, kind="ExternalOutput").ap())
    program(nc, *args)
    r = _run(nc, [arrays], core_ids=[0])
    got = tuple(r.results[0][f"out_{i}_dram"] for i in range(len(_OUTS)))
    return got[0]
```

```python
from contextlib import ExitStack

import concourse.bass as bass
from concourse import mybir

F32 = mybir.dt.float32
I32 = mybir.dt.int32
BF16 = mybir.dt.bfloat16
F8 = mybir.dt.float8e4
ALU = mybir.AluOpType
ACT = mybir.ActivationFunctionType
AX = mybir.AxisListType.X

P = 128
N = 3125
NB = 25
NP = NB * P
LAST = N - (NB - 1) * P
E = 100000
CH = 256
NC = 391
EP = NC * CH
J = EP // P
EFULL = (P - 1) * J
NS = E // CH + NB
N1 = EP // P
NS1 = E // P + NB
SLOT = 264
NG = (J + 15) // 16
GW = 20 * P
D = 256
BIG = 1.0e30
EPS = 1e-5


class Eng:

    def __init__(self, sem):
        self.sem, self.n, self.q, self.seen = sem, 0, [], {}

    def need(self, *toks):
        for t in toks:
            if t is None:
                continue
            sem, v = t
            if self.seen.get(id(sem), 0) < v:
                self.seen[id(sem)] = v
                self.q.append(lambda e, sem=sem, v=v: e.wait_ge(sem, v))

    def do(self, f, *toks):
        self.need(*toks)
        self.n += 1
        self.q.append(lambda e: f(e).then_inc(self.sem, 1))
        return self.sem, self.n

    def raw(self, f, *toks):
        self.need(*toks)
        self.q.append(f)

    def replay(self, e):
        for f in self.q:
            f(e)


class Landing:

    def __init__(self, sem):
        self.sem, self.n = sem, 0

    def go(self, eng, f, *toks):
        eng.need(*toks)
        self.n += 16
        eng.q.append(lambda e: f(e).then_inc(self.sem, 16))
        return self.sem, self.n


def program(nc, x, src, dst, ew, w1, b1, g1, be1, w2, b2, g2, be2, wp, bp,
            gw1, al1, ar1, gw2, al2, ar2, out):
    ctx = ExitStack()
    with ctx:
        def sb(name, shape, dt=F32):
            return ctx.enter_context(nc.sbuf_tensor(name, shape, dt))

        def psum(name, shape):
            return ctx.enter_context(nc.psum_tensor(name, shape, F32))

        def sem(name):
            return ctx.enter_context(nc.semaphore(name))

        def dram(name, shape, dt=F32):
            return nc.dram_tensor(name, shape, dt).ap()

        V, T, A, G, S = (Eng(sem(f"s_{n}")) for n in "vtags")
        lands = {}

        def land(name):
            if name not in lands:
                lands[name] = Landing(sem(f"l_{name}"))
            return lands[name]

        t0 = dram("t0", [NP, D])
        t1 = dram("t1", [NP, D])
        t2 = dram("t2", [NP, 520])
        t3 = dram("t3", [NP, D])
        el_d = dram("el_d", [NP, 8])
        el2_d = dram("el2_d", [NP, 1])
        h_d = dram("h_d", [EP, 8])
        h2_d = dram("h2_d", [EP, 1])
        ex_d = dram("ex_d", [NC, P, 16])
        ex2_d = dram("ex2_d", [N1, P])
        tab_d = dram("tab_d", [N1, 3 * P], I32)
        edp_d = dram("edp_d", [EP + 2], I32)
        trlo_d = dram("trlo_d", [16 * NG, P], BF16)
        trhi_d = dram("trhi_d", [16 * NG, P], BF16)
        ot_d = dram("ot_d", [P, NG * GW], F8)

        a0 = sb("a0", [P, 13000])
        a1 = sb("a1", [P, NB, D])
        xres = sb("xres", [P, NB, D])
        a3 = sb("a3", [P, 6400])
        src_n = sb("src_n", [P, J], I32)
        dst_n = sb("dst_n", [P, J], I32)
        last = sb("last", [1, 3 * P], I32)
        negh = sb("negh", [P, J])
        negt = sb("negt", [P, J])
        dl1 = sb("dl1", [P, 896])
        wsl = sb("wsl", [P, 896])
        src1 = sb("src1", [P, 896], I32)
        ndl = sb("ndl", [P, 2, 512])
        srci = sb("srci", [P, 2, 512], I32)
        br = sb("br", [4, P], I32)
        br1 = sb("br1", [7, P], I32)
        cr = sb("cr", [4, P], I32)
        wts = sb("wts", [P, 4384])
        w1s, w2s, wps = (wts[:, 512 * i:512 * (i + 1)].rearrange("p (k n) -> p k n", k=2) for i in range(3))
        gw1s = wts[:, 1536:2592].rearrange("p (k n) -> p k n", k=2)
        vec = wts[:, 2592:4384].rearrange("p (k n) -> p k n", k=7)
        gw2s = sb("gw2s", [P, 4, 258])
        att1 = a0[:, 6400:7424].rearrange("p (i n) -> p i n", i=2)
        att2 = a0[:, 7424:7936].rearrange("p (i n) -> p i n", i=2)
        iota = sb("iota", [P, P])
        iotab = sb("iotab", [P, P], BF16)
        ident = sb("ident", [P, P])
        ones = sb("ones", [P, P])
        upper = sb("upper", [P, P])
        ioc = sb("ioc", [P, 32])
        sio = sb("sio", [P, 7])
        pidx = sb("pidx", [P, 1])
        kidx = sb("kidx", [P, 1])
        small = sb("small", [P, 512])
        smalli = sb("smalli", [P, 80], I32)
        ends = sb("ends", [1, 2], I32)
        oh = sb("oh", [P, 4, 2, P])
        oht = sb("oht", [P, 2, P])
        exb = sb("exb", [P, 8, 16])
        yt = sb("yt", [P, 2, 512])
        stat = sb("stat", [P, NB, 6])
        mv = sb("mv", [P, NB, 2])
        rstd = sb("rstd", [P, NB])
        nmr = sb("nmr", [P, NB])
        nmu = sb("nmu", [P, NB])
        mhalf = sb("mhalf", [P, 1])
        elr = sb("elr", [P, NB, 16])
        den = sb("den", [P, NB, 8])
        sidx = sb("sidx", [P, NB], I32)
        deg = sb("deg", [P, NB])
        acol = sb("acol", [P, 4])
        ct = sb("ct", [8, 2, P + 1])
        pas = sb("pas", [8, 2, P])
        cin = sb("cin", [P, 2, 8])

        ps = psum("ps", [P, 8 * 512])
        pbig = [ps[:, 1024 * i:1024 * (i + 1)] for i in range(3)]
        tp = [ps[:, 512 * i:512 * (i + 1)] for i in (4, 5)]
        mp = [ps[:, 512 * i:512 * (i + 1)] for i in (6, 7)]

        def bc(ap, shape):
            return ap.to_broadcast(shape)

        c_i = G.do(lambda e: e.iota(iota[:, :], [[1, P]], base=0, channel_multiplier=0, allow_small_or_imprecise_dtypes=True))
        c_ib = G.do(lambda e: e.iota(iotab[:, :], [[1, P]], base=0, channel_multiplier=0, allow_small_or_imprecise_dtypes=True))
        c_ic = G.do(lambda e: e.iota(ioc[:, :], [[1, 32]], base=0, channel_multiplier=0, allow_small_or_imprecise_dtypes=True))
        c_s = G.do(lambda e: e.iota(sio[:, :], [[P, 7]], base=0, channel_multiplier=1, allow_small_or_imprecise_dtypes=True))
        c_pi = G.do(lambda e: e.iota(pidx[:, :], [[1, 1]], base=0, channel_multiplier=1, allow_small_or_imprecise_dtypes=True))
        c_mh = G.do(lambda e: e.memset(mhalf[:, :], -0.5))
        c_z = G.do(lambda e: e.memset(ident[:, :], 0.0))
        c_id = G.do(lambda e: e.affine_select(out=ident[:, :], in_=ident[:, :], compare_op=ALU.not_equal, fill=1.0, base=0,
                                              pattern=[[-1, P]], channel_multiplier=1), c_z)
        c_on = G.do(lambda e: e.memset(ones[:, :], 1.0))
        c_zu = G.do(lambda e: e.memset(upper[:, :], 0.0))
        c_up = G.do(lambda e: e.affine_select(out=upper[:, :], in_=upper[:, :], compare_op=ALU.is_ge, fill=1.0, base=0,
                                              pattern=[[-1, P]], channel_multiplier=1), c_zu)
        ce = G.do(lambda e: e.memset(ends[:, 0:1], -1))
        ce = G.do(lambda e: e.memset(ends[:, 1:2], 5000), ce)

        m1 = V.do(lambda e: e.memset(dst_n[:, :], 4000))
        m2 = V.do(lambda e: e.memset(src_n[:, :], 0))
        V.do(lambda e: e.memset(last[:, :], 0))
        m3 = V.do(lambda e: e.memset(last[:, P:2 * P], 4000), (V.sem, V.n))
        m4 = V.do(lambda e: e.memset(xres[:, NB - 1, :], 0.0))

        def nat(t, d, name, dep):
            lt = None
            for lo, p0, pn in ((0, 0, P - 1), (EFULL, P - 1, 1)):
                n = J if pn > 1 else E - EFULL
                lt = land(name).go(S, lambda e, lo=lo, p0=p0, pn=pn, n=n: e.dma_start(
                    t[p0:p0 + pn, 0:n], d[lo:lo + pn * n].rearrange("(p n) -> p n", n=n)), dep)
            return lt

        d_dst = nat(dst_n, dst, "dst", m1)
        half = 12
        d_x = land("x").go(S, lambda e: e.dma_start(xres[:, 0:half, :], x[0:half * P, :].rearrange("(b p) n -> p b n", p=P)))
        full = E // P
        for i, d in enumerate((src, dst, ew)):
            o = tab_d if i < 2 else tab_d.bitcast(F32)
            land("tab").go(S, lambda e, i=i, d=d, o=o: e.dma_start(o[0:full, P * i:P * (i + 1)], d[0:full * P].rearrange("(c k) -> c k", k=P)))
            lo_ = last[:, P * i:P * i + E - full * P]
            lo_ = lo_ if i < 2 else lo_.bitcast(F32)
            d_last = land("last").go(S, lambda e, d=d, lo_=lo_: e.dma_start(lo_, d[full * P:E].rearrange("(o n) -> o n", o=1)), m3)
        d_tab = land("tab").go(S, lambda e: e.dma_start(tab_d[full:N1, :], last[:, :]), d_last)
        d_src = nat(src_n, src, "src", m2)
        land("x").go(S, lambda e: e.dma_start(xres[:, half:NB - 1, :], x[half * P:(NB - 1) * P, :].rearrange("(b p) n -> p b n", p=P)))
        d_x = land("x").go(S, lambda e: e.dma_start(xres[0:LAST, NB - 1, :], x[(NB - 1) * P:N, :]), m4)
        land("edp").go(S, lambda e: e.dma_start(edp_d[1:EP + 1].rearrange("(p n) -> p n", n=J), dst_n[:, :]), d_dst)
        land("edp").go(S, lambda e: e.dma_start(edp_d[0:1].rearrange("(p n) -> p n", n=1), ends[:, 0:1]), ce)
        d_edp = land("edp").go(S, lambda e: e.dma_start(edp_d[EP + 1:EP + 2].rearrange("(p n) -> p n", n=1), ends[:, 1:2]), ce)
        for t, d in ((w1s, w1), (w2s, w2), (wps, wp)):
            d_wt = land("wt").go(S, lambda e, t=t, d=d: e.dma_start(t[:, :, :], d.rearrange("(k p) n -> p k n", p=P)))
        land("wt").go(S, lambda e: e.dma_start(gw1s[:, :, 0:512], gw1.rearrange("(k p) n -> p k n", p=P)))
        land("wt").go(S, lambda e: e.dma_start(gw2s[:, :, 0:D], gw2.rearrange("(k p) n -> p k n", p=P)))
        for i, d in enumerate((b1, g1, be1, b2, g2, be2, bp)):
            d_wt = land("wt").go(S, lambda e, i=i, d=d: e.dma_start(vec[:, i, :], d.rearrange("(o n) -> o n", o=1).to_broadcast([P, D])))
        for i, d in enumerate((al1, ar1)):
            land("att").go(S, lambda e, i=i, d=d: e.dma_start(
                att1[:, i, :], d.rearrange("h d -> (h d)").rearrange("(o n) -> o n", o=1).to_broadcast([P, 512])))
        for i, d in enumerate((al2, ar2)):
            d_att = land("att").go(S, lambda e, i=i, d=d: e.dma_start(att2[:, i, :], d.to_broadcast([P, D])))

        def stats(b, ap, *deps):
            s = V.do(lambda e: e.bn_stats(stat[:, b, :], ap), *deps)
            return V.do(lambda e: e.bn_aggr(mv[:, b, :], stat[:, b, :]), s)

        def norm(b, o, i, func, *deps):
            return A.do(lambda e: e.activation(o, i, func, bias=nmr[:, b:b + 1], scale=rstd[:, b:b + 1]), *deps)

        def scale(b, dep, n=1):
            r, m, q = (t[:, b:b + n] for t in (rstd, nmu, nmr))
            g = G.do(lambda e: e.tensor_scalar(r, mv[:, b:b + n, 1], EPS, None, ALU.add), dep)
            G.do(lambda e: e.tensor_scalar(m, mv[:, b:b + n, 0], -1.0, None, ALU.mult))
            g = G.do(lambda e: e.tensor_tensor(r, r, bc(mhalf[:, :], [P, n]), ALU.pow), g, c_mh)
            return G.do(lambda e: e.tensor_tensor(q, m, r, ALU.mult), g)

        def pipeline(*stages):
            for i in range(NB + max(lag for lag, _ in stages)):
                for lag, f in sorted(stages, key=lambda st: -st[0]):
                    if 0 <= i - lag < NB:
                        f(i - lag)

        GRP = 5

        def store(t, name, b, tok):
            if b % GRP == GRP - 1:
                return land(name).go(S, lambda e: e.dma_start(
                    t[(b - GRP + 1) * P:(b + 1) * P, :].rearrange("(b p) n -> p b n", p=P), a1[:, b - GRP + 1:b + 1, :]), tok)
            return None

        cnt = small[:, 0:NB]
        junk = a3[:, 0:J]
        SPLIT = 13
        c0 = V.do(lambda e: e.memset(cnt, 0.0))
        v = V.do(lambda e: e.tensor_scalar(small[:, 32:32 + NB], ioc[:, 0:NB], float(P), -0.5, ALU.mult, ALU.add), c_ic)
        c1 = v
        for b in range(1, NB):
            if b < SPLIT:
                c0 = V.do(lambda e, b=b: e.tensor_scalar(junk, dst_n[:, :], float(P * b), None, ALU.is_lt, ALU.add,
                                                         accum_out=small[:, b:b + 1]), d_dst, c0)
            else:
                c1 = A.do(lambda e, b=b: e.activation(a3[:, 800:800 + J], dst_n[:, :], ACT.Sign, bias=small[:, 32 + b:33 + b], scale=-1.0,
                                                      accum_out=small[:, 64 + b:65 + b]), d_dst, c1)
        c0 = V.do(lambda e: e.tensor_scalar(small[:, SPLIT:NB], small[:, 64 + SPLIT:64 + NB], float(J), 0.5, ALU.add, ALU.mult), c0, c1)
        eb = T.do(lambda e: e.matmul(tp[0][:, 0:NB], ones[:, :], cnt, start=True, stop=True), c0, c_on)
        v_cnt = V.do(lambda e: e.tensor_copy(smalli[:, 0:NB], tp[0][:, 0:NB]), eb)

        def plan(sh, n, top, o, ci, dep):
            v = V.do(lambda e: e.tensor_scalar(smalli[:, 32:32 + NB], smalli[:, 0:NB], sh, None, ALU.arith_shift_right), dep)
            v = V.do(lambda e: e.tensor_copy(small[:, 32:32 + NB], smalli[:, 32:32 + NB]), v)
            v = V.do(lambda e: e.tensor_tensor(small[:, 64:64 + NB], small[:, 32:32 + NB], ioc[:, 0:NB], ALU.add), v, c_ic)
            cmp = small[:, 128:128 + 24 * n].rearrange("p (k b) -> p k b", k=n)
            v = V.do(lambda e: e.tensor_tensor(cmp, bc(sio[:, 0:n].rearrange("p (k o) -> p k o", o=1), [P, n, 24]),
                                               bc(small[:, 65:65 + 24].rearrange("p (o b) -> p o b", o=1), [P, n, 24]),
                                               ALU.is_ge), v, c_s)
            bs, cs, nbs = (small[:, o + 8 * i:o + 8 * i + n] for i in range(3))
            v = V.do(lambda e: e.tensor_reduce(bs, cmp, AX, ALU.add), v)
            V.do(lambda e: e.tensor_scalar(nbs, bs, -128.0, None, ALU.mult), v)
            v = V.do(lambda e: e.tensor_tensor(cs, sio[:, 0:n], bs, ALU.subtract), v)
            v = V.do(lambda e: e.tensor_scalar(cs, cs, float(top - 1), None, ALU.min), v)
            return V.do(lambda e: e.tensor_copy(smalli[:, ci:ci + n], cs), v)

        v_ci = plan(7, 7, N1, 304, 60, v_cnt)
        rows = a0[:, 0:2688].bitcast(I32).rearrange("p (k w) -> p k w", k=7)
        for k in range(7):
            r_in = land("rows").go(G, lambda e, k=k: e.indirect_dma_start(
                out=rows[:, k, :], out_offset=None, in_=tab_d,
                in_offset=bass.IndirectOffsetOnAxis(ap=smalli[:, 60 + k:61 + k], axis=0)), d_tab, v_ci)
        K0 = {}

        def first_stats(b):
            v = stats(b, xres[:, b, :], d_x)
            if b % GRP == GRP - 1:
                K0[b // GRP] = scale(b - GRP + 1, v, GRP)

        def first_norm(b):
            K0["a"] = norm(b, a1[:, b, :], xres[:, b, :], ACT.Relu, K0[b // GRP])
            store(t0, "t0", b, K0["a"])

        pipeline((0, first_stats), (GRP, first_norm))

        rsf = a0[:, 2688:3584]
        rdf = a0[:, 3584:4480]
        v_rs = V.do(lambda e: e.tensor_copy(rsf.rearrange("p (k w) -> p k w", k=7), rows[:, :, 0:P]), r_in)
        for k in range(7):
            v_rd = V.do(lambda e, k=k: e.tensor_scalar(rdf[:, P * k:P * (k + 1)], rows[:, k, P:2 * P], small[:, 320 + k:321 + k], None, ALU.add), v_ci)
        banks = tp + mp
        bank_free = [None] * 4
        used = [0]
        rwf = a0[:, 0:2688].rearrange("p (k w) -> p k w", k=7)[:, :, 2 * P:3 * P]
        parts = ((lambda k: rsf[:, P * k:P * (k + 1)], v_rs, src1), (lambda k: rdf[:, P * k:P * (k + 1)], v_rd, dl1),
                 (lambda k: rwf[:, k, :], v_rd, wsl))

        def to_slots(f, dep, tab):
            for k0, k1 in ((0, 4), (4, 7)):
                i = used[0] % 4
                used[0] += 1
                for k in range(k0, k1):
                    t = T.do(lambda e, k=k, i=i, k0=k0: e.transpose(banks[i][:, P * (k - k0):P * (k - k0 + 1)], f(k), ident[:, :]), dep, c_id, bank_free[i], v_cnt)
                bank_free[i] = slot_copy(tab, i, k0, k1, t)
            return bank_free[i]

        def slot_copy(tab, i, k0, k1, t):
            return V.do(lambda e: e.tensor_copy(tab[:, P * k0:P * k1], banks[i][:, 0:P * (k1 - k0)]), t)

        for f, dep, tab in parts:
            v_tab = to_slots(f, dep, tab)
        t = T.do(lambda e: e.transpose(banks[0][0:7, 0:P], small[:, 304:311], ident[:, :]), v_tab)
        v_reg = V.do(lambda e: e.tensor_copy(br1[:, :], banks[0][0:7, 0:P]), t)

        NR = 10
        ring_free = [None] * NR
        oh_free = [None] * 4
        ps_free = [None] * 3
        ex_free = [None] * 8
        regs = {}

        def block_of(e, s, br):
            if s % 4 == 0:
                if "b" not in regs:
                    regs["b"] = [e.alloc_register(f"rb{i}") for i in range(4)]
                k = s // P
                e.load(regs["b"], br[k:k + 1, s % P:s % P + 4])
            return e.snap(regs["b"][s % 4], min_val=0, max_val=NB - 1)

        def chunk_of(e, s):
            if s % 4 == 0:
                if "c" not in regs:
                    regs["c"] = [e.alloc_register(f"rc{i}") for i in range(4)]
                k = s // P
                e.load(regs["c"], cr[k:k + 1, s % P:s % P + 4])
            return e.snap(regs["c"][s % 4], min_val=0, max_val=NC - 1)

        NR1 = 24
        ring1 = [None] * NR1
        oh1_free = [None] * 8
        ps1_free = [None] * 6

        def aggregate(table, W, acc, start, side=None, ahead=None, weights=None):
            def gather(s):
                return land(f"g{s % NR1}").go(G, lambda e: e.indirect_dma_start(
                    out=a3[:, SLOT * (s % NR1):SLOT * (s % NR1) + D], out_offset=None, in_=table,
                    in_offset=bass.IndirectOffsetOnAxis(ap=src1[:, s:s + 1], axis=0)), ring1[s % NR1], ahead or start, v_tab)

            early = [gather(s) for s in range(11)] if weights else []
            ready = weights() if weights else v_tab
            pend = []
            done = start
            for s in range(NS1):
                r, so = s % NR1, s % 8
                buf = a3[:, SLOT * r:SLOT * r + W]
                g_in = early[s] if s < len(early) else gather(s)
                o = oh[:, so // 2, so % 2, :]
                ok = V.do(lambda e, s=s, o=o: e.tensor_scalar(o, iota[:, :], dl1[:, s:s + 1], wsl[:, s:s + 1], ALU.is_equal, ALU.mult),
                          ready, c_i, oh1_free[so])
                if len(pend) == 4:
                    done = pend.pop(0)()
                pp = ps[:, 512 * (s % 6):512 * (s % 6) + W]
                t = T.do(lambda e, pp=pp, o=o, buf=buf: e.matmul(pp, o, buf, start=True, stop=True), ok, g_in, ps1_free[s % 6])
                ring1[r] = oh1_free[so] = t

                def evac(s=s, t=t, pp=pp):
                    def add(e):
                        b = block_of(e, s, br1)
                        d = acc[:, bass.ds(b * W, W)]
                        return e.tensor_tensor(d, d, pp, ALU.add)
                    tok = V.do(add, t, done, v_reg)
                    ps1_free[s % 6] = tok
                    return tok
                pend.append(evac)
                if side is not None and s % 2 == 0:
                    side(s // 2)
            for f in pend:
                done = f()
            return done

        def aggregate_heads(table, acc, start, ahead, before_sums):
            W = 520
            rows = [a3[:, W * i:W * (i + 1)] for i in range(12)] + [wts[:, W * i:W * (i + 1)] for i in range(8)]

            def gather(s):
                for k in range(2):
                    g_in = gather_one(s, k)
                return g_in

            def gather_one(s, k):
                r = s % NR
                return land(f"g{r}").go(G, lambda e: e.indirect_dma_start(
                    out=rows[2 * r + k], out_offset=None, in_=table,
                    in_offset=bass.IndirectOffsetOnAxis(ap=srci[:, k, s:s + 1], axis=0)), ring_free[r], ahead, v_slots2)

            early = [gather(s) for s in range(NR)]
            before_sums()
            pend = []
            done = start
            for s in range(NS):
                r = s % NR
                buf = rows[2 * r:2 * r + 2]
                q = s % 8
                x_in = land(f"ex{q}").go(S, lambda e, s=s, q=q: e.dma_start(
                    exb[:, q, :], ex_d[bass.ds(chunk_of(e, s), 1), :, :].rearrange("o p f -> (o p) f")), ex_free[q], start, v_slots2)
                g_in = early[s] if s < len(early) else gather(s)
                so = s % 4
                oks = []
                for k in range(2):
                    o = oh[:, so, k, :]
                    a = A.do(lambda e, s=s, k=k: e.activation(oht[:, k, :], iota[:, :], ACT.Abs, bias=ndl[:, k, s:s + 1]),
                             v_slots2, c_i, oh_free[so])
                    ok = A.do(lambda e, k=k, o=o: e.activation(o, oht[:, k, :], ACT.Relu, bias=1.0, scale=-1.0), a)
                    oks.append(ok)
                for k in range(2):
                    bv = buf[k].rearrange("p (h d) -> p h d", h=8)
                    mk = V.do(lambda e, k=k, bv=bv, s=s: e.tensor_tensor(
                        bv, bv, bc(exb[:, s % 8, 8 * k:8 * k + 8].rearrange("p (h o) -> p h o", o=1), [P, 8, 65]), ALU.mult), g_in, x_in)
                    oks.append(mk)
                if len(pend) == 2:
                    done = pend.pop(0)()
                pp = pbig[s % 3]
                t = None
                for u in range(2):
                    for k in range(2):
                        t = T.do(lambda e, pp=pp, so=so, k=k, u=u, buf=buf: e.matmul(
                            pp[:, 512 * u:512 * u + 260], oh[:, so, k, :], buf[k][:, 260 * u:260 * (u + 1)], start=(k == 0), stop=(k == 1)),
                            *oks, g_in, ps_free[s % 3])
                ring_free[r] = t
                oh_free[so] = t
                ex_free[s % 8] = t

                def evac(s=s, t=t, pp=pp):
                    def add(e):
                        b = block_of(e, s, br)
                        d = acc[:, bass.ds(b * W, W)]
                        d = d.rearrange("p (u w) -> p u w", u=2)
                        return e.tensor_tensor(d, d, pp.rearrange("p (u w) -> p u w", u=2)[:, :, 0:260], ALU.add)
                    tok = V.do(add, t, done, v_slots2)
                    ps_free[s % 3] = tok
                    return tok
                pend.append(evac)
            for f in pend:
                done = f()
            return done

        dn = [0]
        tfree, yfree = [None, None], {}
        pfree = [None] * 8

        def bank(i):
            return ps[:, 512 * i:512 * (i + 1)]

        def turn(inp, K, y, slot, dep, shift=0.0):
            i = dn[0] % 2
            dn[0] += 1
            for k in range(K):
                t = T.do(lambda e, k=k: e.transpose(tp[i][:, P * k:P * (k + 1)], inp[:, P * k:P * (k + 1)], ident[:, :]),
                         dep, c_id, tfree[i])
            c = A.do(lambda e: e.activation(y, tp[i][:, 0:P * K], ACT.Copy, bias=shift), t, yfree.get(slot))
            tfree[i] = c
            return c

        def multiply(y, slot, K, ws, Nc, dep, pb, extra=0, bias=None):
            for k in range(K):
                t = T.do(lambda e, k=k: e.matmul(bank(pb)[:, 0:Nc], y[:, P * k:P * (k + 1)], ws[:, k, 0:Nc],
                                                 start=(k == 0), stop=(k == K - 1 and bias is None)), dep, d_wt, pfree[pb])
            if bias is not None:
                t = T.do(lambda e: e.matmul(bank(pb)[:, 0:Nc], ones[0:1, :], bias, start=False, stop=True))
            if extra:
                for k in range(K):
                    t = T.do(lambda e, k=k: e.matmul(bank(1)[:, 0:extra], y[:, P * k:P * (k + 1)], ws[:, k, Nc:Nc + extra],
                                                     start=(k == 0), stop=(k == K - 1)), pfree[1])
            yfree[slot] = t
            return t

        def ysl(slot, K=2):
            return yt[:, :, :].rearrange("p u n -> p (u n)")[:, P * K * slot:P * K * (slot + 1)]

        a1f = a1[:, :, :].rearrange("p b n -> p (b n)")
        hb = a0[:, 6400:12800].rearrange("p (b n) -> p b n", n=D)

        lo = a0[:, 0:J]
        hi = a0[:, 800:800 + J]
        dti = a0[:, 1600:1600 + J].bitcast(I32)
        ohl = a0[:, 2400:2400 + 2 * 1024].bitcast(BF16).rearrange("p (u j d) -> p u j d", u=2, j=16)
        ohh = a0[:, 5000:5000 + 2 * 256].bitcast(BF16).rearrange("p (u j d) -> p u j d", u=2, j=16)
        hst = {"free": [None, None], "t": None}

        def bits():
            v = V.do(lambda e: e.tensor_scalar(dti, dst_n[:, :], 127, None, ALU.bitwise_and), v_reg)
            v = V.do(lambda e: e.tensor_copy(lo, dti), v)
            v = V.do(lambda e: e.tensor_scalar(dti, dst_n[:, :], 7, None, ALU.arith_shift_right), v)
            hst["v"] = V.do(lambda e: e.tensor_copy(hi, dti), v)

        def histogram(s):
            if s % 8 == 0 and s // 8 < NB:
                b = s // 8
                hst["x"] = V.do(lambda e: e.tensor_tensor(xres[:, b, :], xres[:, b, :], vec[:, 6, :], ALU.add), K0["a"], d_wt)
            if s % 8 != 4 or s // 8 >= 49:
                return
            g = s // 8
            j0, jn = 16 * g, min(16, J - 16 * g)
            u = g % 2
            v1 = V.do(lambda e: e.tensor_tensor(ohl[:, u, 0:jn, :], bc(iotab[:, :].rearrange("p (o d) -> p o d", o=1), [P, jn, P]),
                                                bc(lo[:, j0:j0 + jn].rearrange("p (j o) -> p j o", o=1), [P, jn, P]), ALU.is_equal),
                      c_ib, hst["v"], hst["free"][u])
            v2 = V.do(lambda e: e.tensor_tensor(ohh[:, u, 0:jn, 0:NB], bc(iotab[:, 0:NB].rearrange("p (o d) -> p o d", o=1), [P, jn, NB]),
                                                bc(hi[:, j0:j0 + jn].rearrange("p (j o) -> p j o", o=1), [P, jn, NB]), ALU.is_equal))
            for i in range(jn):
                t = T.do(lambda e, i=i: e.matmul(mp[0][:, 0:NB], ohl[:, u, i, :], ohh[:, u, i, 0:NB],
                                                 start=(j0 + i == 0), stop=(j0 + i == J - 1)), v2)
            hst["free"][u] = hst["t"] = t

        dpn = a0[:, 10100:10100 + J].bitcast(I32)
        dnn = a0[:, 10900:10900 + J].bitcast(I32)
        zer = a0[:, 8448:8448 + 2 * J]
        ftmp = a0[:, 7936:8448]
        slo = a0[:, 11700:11700 + J]
        shi = a0[:, 5600:5600 + J]
        sti = a0[:, 10100:10100 + J].bitcast(I32)
        trb = [a0[:, o:o + 448].bitcast(BF16).rearrange("p (g e) -> p g e", e=P) for o in (10900, 12490)]
        M = {}
        jobs = []

        def job(f):
            jobs.append(f)

        def zeros():
            z = V.do(lambda e: e.memset(zer, -BIG), v_reg)
            hz = h_d.rearrange("e h -> (e h)").rearrange("(p n) -> p n", p=P)
            for i in range(4):
                land("hz").go(S, lambda e, i=i: e.dma_start(hz[:, 2 * J * i:2 * J * (i + 1)], zer), z)
            M["hz"] = land("hz").go(S, lambda e: e.dma_start(h2_d.rearrange("e h -> (e h)").rearrange("(p n) -> p n", p=P), zer[:, 0:J]), z)
            land("dp").go(S, lambda e: e.dma_start(dpn, edp_d[0:EP].rearrange("(p n) -> p n", n=J)), d_edp, v_reg)
            M["dp"] = land("dp").go(S, lambda e: e.dma_start(dnn, edp_d[2:EP + 2].rearrange("(p n) -> p n", n=J)), d_edp, v_reg)

        job(zeros)

        def k_index():
            v = V.do(lambda e: e.tensor_scalar(small[:, 480:483], ioc[:, 1:4], 25.0, None, ALU.mult), c_ic)
            v = V.do(lambda e: e.tensor_tensor(small[:, 484:487], bc(pidx[:, :], [P, 3]), small[:, 480:483], ALU.is_ge), v, c_pi)
            v = V.do(lambda e: e.tensor_reduce(small[:, 488:489], small[:, 484:487], AX, ALU.add), v)
            M["k"] = V.do(lambda e: e.scalar_tensor_tensor(out=kidx[:, :], in0=small[:, 488:489], scalar=-25.0, in1=pidx[:, :],
                                                           op0=ALU.mult, op1=ALU.add), v)

        job(k_index)

        def fold(g, at, k, i, n, c, H):
            def f():
                v = V.do(lambda e: e.tensor_tensor(ftmp[:, 0:n], g[:, k, 0:n], at[:, i, :], ALU.mult), d_wt, d_att, M.get("f"))
                M["f"] = V.do(lambda e: e.tensor_reduce(g[:, k, c:c + H], ftmp[:, 0:n].rearrange("p (h d) -> p h d", h=H), AX, ALU.add), v)
            return f

        for i in range(2):
            for k in range(2):
                job(fold(gw1s, att1, k, i, 512, 512 + 8 * i, 8))
            for k in range(4):
                job(fold(gw2s, att2, k, i, D, D + i, 1))

        def same(q, d):
            def f():
                M["q", id(q)] = V.do(lambda e: e.tensor_tensor(q[:, :], dst_n[:, :], d, ALU.is_equal), M["dp"])
            return f

        def neg(o, q):
            def f():
                M["q", id(o)] = V.do(lambda e: e.tensor_scalar(o[:, :], q[:, :], BIG, -BIG, ALU.mult, ALU.add), M["q", id(q)])
            return f

        def least(i, q):
            def f():
                M["fl"] = V.do(lambda e: e.tensor_reduce(acol[:, i:i + 1], q[:, :], AX, ALU.min), M["q", id(q)])
            return f

        def passing():
            for i in range(2):
                t = T.do(lambda e, i=i: e.transpose(mp[1][0:8, P * i:P * (i + 1)], bc(acol[:, i:i + 1], [P, 8]), ident[:, :]), M["fl"])
            v = V.do(lambda e: e.tensor_copy(pas[:, :, :], mp[1][0:8, 0:2 * P].rearrange("p (i n) -> p i n", i=2)), t)
            M["t"] = v
            V.do(lambda e: e.memset(ct[:, 0, 0:1], -BIG))
            M["pas"] = V.do(lambda e: e.memset(ct[:, 1, P:P + 1], -BIG))

        job(same(negh, dpn))
        job(same(negt, dnn))
        job(neg(negh, negh))
        job(neg(negt, negt))
        for i, q in enumerate((negh, negt)):
            job(least(i, q))
        job(passing)

        def source_bits(op, n, o):
            def f():
                v = V.do(lambda e: e.tensor_scalar(sti, src_n[:, :], n, None, op), M.get("b"), M["fl"], d_src)
                M["b"] = M["bits", n] = V.do(lambda e: e.tensor_copy(o, sti), v)
            return f

        def source_rows(o, n, w, g0, g1):
            def f():
                for g in range(g0, g1):
                    m = min(P, J - P * g)
                    t = T.do(lambda e, g=g, m=m: e.transpose(mp[1][0:m, P * (g - g0):P * (g - g0 + 1)], o[:, P * g:P * g + m], ident[:, :]),
                             M["bits", n], M.get("t"))
                for g in range(g0, g1):
                    m = min(P, J - P * g)
                    v = V.do(lambda e, g=g, m=m: e.tensor_copy(trb[w][0:m, g, :], mp[1][0:m, P * (g - g0):P * (g - g0 + 1)]), t, M.get("p"))
                M["t"] = v
            return f

        def pad():
            V.do(lambda e: e.memset(trb[0][:, 6, :], 0.0), M["fl"])
            M["p"] = V.do(lambda e: e.memset(trb[1][:, 6, :], 0.0))

        def rows_out(w, d):
            def f():
                land("tr").go(S, lambda e: e.dma_start(d[0:6 * P, :].rearrange("(g j) e -> j g e", j=P), trb[w][:, 0:6, :]), M["t"])
                M["tr"] = land("tr").go(S, lambda e: e.dma_start(d[6 * P:16 * NG, :], trb[w][0:16 * NG - 6 * P, 6, :]))
            return f

        def plan2():
            M["ci2"] = plan(8, 4, NC, 336, 67, v_cnt)

        job(plan2)
        job(pad)
        for w, (op, n, o, d) in enumerate(((ALU.bitwise_and, 127, slo, trlo_d), (ALU.arith_shift_right, 7, shi, trhi_d))):
            job(source_bits(op, n, o))
            job(source_rows(o, n, w, 0, 4))
            job(source_rows(o, n, w, 4, 7))
            job(rows_out(w, d))

        rows2 = a0[:, 6400:9472].bitcast(I32).rearrange("p (k u w) -> p k u w", k=4, u=2)
        rf2 = a0[:, 9472:10496].rearrange("p (k w) -> p k w", k=4)

        def rows2_in():
            for k in range(4):
                M["r2"] = land("rows").go(G, lambda e, k=k: e.indirect_dma_start(
                    out=a0[:, 6400 + 768 * k:7168 + 768 * k].bitcast(I32), out_offset=None, in_=tab_d.rearrange("(c u) w -> c (u w)", u=2),
                    in_offset=bass.IndirectOffsetOnAxis(ap=smalli[:, 67 + k:68 + k], axis=0)), M["ci2"], M["f"], M["hz"])

        def slots2(i, tab):
            def f():
                if i == 0:
                    v = V.do(lambda e: e.tensor_copy(rf2.rearrange("p k (u w) -> p k u w", u=2), rows2[:, :, :, 0:P]), M["r2"], M["b"], M["hz"])
                else:
                    for k in range(4):
                        v = V.do(lambda e, k=k: e.tensor_scalar(rf2[:, k, :].rearrange("p (u w) -> p u w", u=2), rows2[:, k, :, P:2 * P],
                                                                small[:, 352 + k:353 + k], None, ALU.add), M["s2"])
                for j in range(2):
                    for k in range(4):
                        t = T.do(lambda e, k=k, j=j: e.transpose(mp[1][:, P * k:P * (k + 1)], rf2[:, k, j:CH:2], ident[:, :]), v, M["t"])
                    if i:
                        M["t"] = V.do(lambda e, j=j: e.tensor_scalar(tab[:, j, :], mp[1][:, :], -1.0, None, ALU.mult), t)
                    else:
                        M["t"] = V.do(lambda e, j=j: e.tensor_copy(tab[:, j, :], mp[1][:, :]), t)
                M["s2"] = M["t"]
            return f

        def registers2():
            for i, tab in enumerate((br, cr)):
                t = T.do(lambda e, i=i: e.transpose(mp[1][0:4, P * i:P * (i + 1)], small[:, 336 + 8 * i:340 + 8 * i], ident[:, :]), M["t"])
            for i, tab in enumerate((br, cr)):
                M["t"] = V.do(lambda e, i=i, tab=tab: e.tensor_copy(tab[:, :], mp[1][0:4, P * i:P * (i + 1)]), t)

        job(rows2_in)
        job(slots2(0, srci))
        job(slots2(1, ndl))
        job(registers2)

        def beside(s):
            histogram(s)
            if s % 4 == 2 and jobs:
                jobs.pop(0)()

        bits()
        d_t0 = land("t0").sem, land("t0").n
        tok = aggregate(t0, D, a1f, d_t0, beside)

        v_slots2 = M["t"]
        v_xb, d_hz, v_pas, d_tr = hst["x"], M["hz"], M["pas"], M["tr"]
        S.need(d_hz)
        V.need(d_hz, d_tr)
        v_dg = V.do(lambda e: e.tensor_copy(deg[:, :], mp[0][:, 0:NB]), hst["t"])
        pfree[6], pfree[7] = v_dg, M["t"]

        def where_edges_begin():
            T.do(lambda e: e.matmul(mp[0][:, 0:NB], ones[:, :], deg[:, :], start=True, stop=True), v_dg, pfree[6])
            t = T.do(lambda e: e.matmul(mp[1][:, 0:NB], upper[:, :], deg[:, :], start=True, stop=True), c_up, pfree[7])
            v = V.do(lambda e: e.tensor_copy(small[:, 0:NB], mp[0][:, 0:NB]), t)
            v = V.do(lambda e: e.tensor_tensor_scan(small[:, 32:32 + NB], ones[:, 0:NB], small[:, 0:NB], 0.0, ALU.mult, ALU.add), v)
            v = V.do(lambda e: e.tensor_tensor(small[:, 64:64 + NB], small[:, 32:32 + NB], small[:, 0:NB], ALU.subtract), v)
            v = V.do(lambda e: e.tensor_tensor(small[:, 64:64 + NB], small[:, 64:64 + NB], mp[1][:, 0:NB], ALU.add), v)
            v = V.do(lambda e: e.tensor_scalar(small[:, 96:96 + NB], deg[:, :], 0.0, 1.0e6, ALU.is_equal, ALU.mult), v)
            v = V.do(lambda e: e.tensor_tensor(small[:, 64:64 + NB], small[:, 64:64 + NB], small[:, 96:96 + NB], ALU.add), v)
            v = V.do(lambda e: e.tensor_copy(sidx[:, :], small[:, 64:64 + NB]), v)
            pfree[6] = pfree[7] = v
            return v

        def conv_stages(tok, ws, ib, last, R, lags, banks=(6, 7)):
            def turned(b):
                R["y", b] = turn(a1[:, b, :], 2, ysl(b % 2), b % 2, tok)

            held = len(banks) > 2

            def product(b):
                R["p", b] = multiply(ysl(b % 2), b % 2, 2, ws, D, R["y", b], banks[b % len(banks)], bias=vec[0:1, ib, :] if held else None)

            def bias(b):
                pb = banks[b % len(banks)]
                if held:
                    R["s", b] = scale(b, stats(b, bank(pb)[:, 0:D], R["p", b]))
                    return
                v = V.do(lambda e: e.tensor_tensor(hb[:, b, :], bank(pb)[:, 0:D], vec[:, ib, :], ALU.add), R["p", b])
                pfree[pb] = v
                R["s", b] = scale(b, stats(b, hb[:, b, :], v))

            def gelu(b):
                pb = banks[b % len(banks)]
                h = bank(pb)[:, 0:D] if held else hb[:, b, :]
                v = V.do(lambda e: e.scalar_tensor_tensor(out=hb[:, b, :], in0=h, scalar=nmu[:, b:b + 1], in1=vec[:, ib + 1, :],
                                                          op0=ALU.add, op1=ALU.mult), R["s", b])
                if held:
                    pfree[pb] = v
                v = V.do(lambda e: e.scalar_tensor_tensor(out=hb[:, b, :], in0=hb[:, b, :], scalar=rstd[:, b:b + 1], in1=vec[:, ib + 2, :],
                                                          op0=ALU.mult, op1=ALU.add), v)
                R["g", b] = A.do(lambda e: e.activation(a1[:, b, :], hb[:, b, :], ACT.Gelu), v)
                if last is not None:
                    store(last, "t1", b, R["g", b])

            return tuple(zip(lags, (turned, product, bias, gelu)))

        RB = {}
        pipeline(*conv_stages(tok, w1s, 0, t1, RB, (0, 2, 3, 5), (6, 7, 0, 1)))
        d_t1 = land("t1").sem, land("t1").n

        obb = a0[:, 6400:8960].bitcast(BF16).rearrange("p (u n) -> p u n", u=2)
        obo = a0[:, 8960:10240].bitcast(F8).rearrange("p (u n) -> p u n", u=2)
        otf = {"b": [None, None], "o": [None, None]}
        v_ob = V.do(lambda e: e.memset(obb[:, :, 16 * P:GW], 0.0), RB["g", NB - 1])

        def one_hots(s):
            if s == 1:
                M["sidx"] = where_edges_begin()
            if s % 8 != 4 or s // 8 >= NG:
                return
            g = s // 8
            u = g % 2
            l = land(f"ob{u}").go(S, lambda e: e.dma_start(obb[:, u, 0:16 * P], trlo_d[16 * g:16 * g + 16, :].rearrange("j e -> (j e)").rearrange(
                "(o n) -> o n", o=1).to_broadcast([P, 16 * P])), d_tr, otf["b"][u], v_ob)
            for t in range(4):
                l = land(f"ob{u}").go(S, lambda e, t=t: e.dma_start(
                    obb[25 * t:25 * t + 25, u, 16 * P:GW].rearrange("k (q e) -> k q e", e=P),
                    trhi_d[16 * g + t:16 * g + 16:4, :].rearrange("(o q) e -> o q e", o=1).to_broadcast([25, 4, P])))
            V.do(lambda e: e.tensor_scalar(obo[:, u, 0:16 * P], obb[:, u, 0:16 * P], pidx[:, :], None, ALU.is_equal, saturate=False), l, c_pi, otf["o"][u])
            v = V.do(lambda e: e.tensor_scalar(obo[:, u, 16 * P:GW], obb[:, u, 16 * P:GW], kidx[:, :], None, ALU.not_equal, saturate=False), M["k"])
            otf["b"][u] = v
            otf["o"][u] = land(f"oo{u}").go(S, lambda e: e.dma_start(ot_d[:, GW * g:GW * (g + 1)], obo[:, u, :]), v)

        T.need(M["f"])

        tok = aggregate(t1, D, a1f, d_t1, one_hots)
        v_sidx = M["sidx"]
        S.need(*otf["o"])
        V.need(*otf["o"])
        A.need(*otf["o"])
        R = {}
        stage = a3[:, 0:2080].rearrange("p (u n) -> p u n", n=520)
        v_st = V.do(lambda e: e.memset(a3[:, 0:2080].rearrange("p (u w) -> p u w", w=65)[:, :, 64:65], 1.0), tok)
        sfree = [None] * 4

        def turn_w(b):
            R["yw", b] = turn(a1[:, b, :], 2, ysl(2), 2, R["g", b])

        def starts(H, b, er, hd, tok):
            return land(f"sc{H}").go(G, lambda e: e.indirect_dma_start(
                out=hd, out_offset=bass.IndirectOffsetOnAxis(ap=sidx[:, b:b + 1], axis=0), in_=er, in_offset=None,
                bounds_check=EP - 1, oob_is_err=False), tok, v_sidx, d_hz)

        def project(b):
            R["w", b] = multiply(ysl(2), 2, 2, wps, D, R["yw", b], 0)

        def residual(b):
            v = V.do(lambda e: e.tensor_tensor(xres[:, b, :], xres[:, b, :], bank(0)[:, 0:D], ALU.add), R["w", b], v_xb)
            pfree[0] = v
            R["n", b] = scale(b, stats(b, xres[:, b, :], v))

        def second_norm(b):
            R["h", b] = norm(b, a1[:, b, :], xres[:, b, :], ACT.Relu, R["n", b])

        def turn_f(b):
            R["yf", b] = turn(a1[:, b, :], 2, ysl(3), 3, R["h", b])

        def features(b):
            R["f", b] = multiply(ysl(3), 3, 2, gw1s, 512, R["yf", b], 2 + b % 2, 16)

        def keep_features(b):
            t = R["f", b]
            u = b % 4
            c = A.do(lambda e: e.activation(stage[:, u, :].rearrange("p (h w) -> p h w", w=65)[:, :, 0:64],
                                            bank(2 + b % 2).rearrange("p (h w) -> p h w", w=64), ACT.Copy), t, sfree[u], v_st)
            R["e"] = V.do(lambda e: e.tensor_copy(elr[:, b, :], bank(1)[:, 0:16]), t)
            pfree[2 + b % 2], pfree[1] = c, R["e"]
            R["sc"] = starts(8, b, elr[:, b, 8:16], h_d, R["e"])
            sfree[u] = land(f"st{u}").go(S, lambda e: e.dma_start(t2[b * P:(b + 1) * P, :], stage[:, u, :]), c)

        pipeline(*conv_stages(tok, w2s, 3, None, R, (0, 1, 2, 4)), (5, turn_w), (6, project), (7, residual),
                 (9, second_norm), (10, turn_f), (11, features), (12, keep_features))
        c = R["e"]
        d_el = land("el").go(S, lambda e: e.dma_start(el_d.rearrange("(b p) h -> p b h", p=P), elr[:, :, 0:8]), c)
        t2_ready = list(sfree)
        for u in range(4):
            ring_free[u] = sfree[u]
        t2_land = c

        def sweep(o, x, f, h, init, back=False, c0=0, c1=J):
            st = -1 if back else 1
            return lambda *dep: V.do(lambda e: e.tensor_tensor_scan(
                o[:, c0:c1, h][:, ::st], f[:, c0:c1][:, ::st], x[:, c0:c1, h][:, ::st], init, ALU.add, ALU.max), *dep)

        def carry(o, H, ways, dep):
            last = None
            t1_ = {}
            for w in ways:
                col = o[:, 0 if w else J - 1, :]
                t1_[w] = T.do(lambda e, w=w, col=col: e.transpose(mp[w][0:H, 0:P], col, ident[:, :]), dep)
            for w in ways:
                a = slice(None, None, -1 if w else 1)
                dst_ = ct[0:H, 1, 0:P] if w else ct[0:H, 0, 1:P + 1]
                t1_[w] = V.do(lambda e, w=w, a=a, dst_=dst_: e.tensor_tensor_scan(
                    dst_[:, a], pas[0:H, w, :][:, a], mp[w][0:H, 0:P][:, a], -BIG, ALU.add, ALU.max), t1_[w], v_pas)
            for w in ways:
                c = ct[0:H, 1, 1:P + 1] if w else ct[0:H, 0, 0:P]
                t1_[w] = T.do(lambda e, w=w, c=c: e.transpose(mp[w][:, 256:256 + H], c, ident[0:H, 0:H]), t1_[w])
            for w in ways:
                last = V.do(lambda e, w=w: e.tensor_copy(cin[:, w, 0:H], mp[w][:, 256:256 + H]), t1_[w])
            return last

        tbl = sb("tbl", [P, 3, 200], BF16)

        def lookup(H, elv, el_sb, groups, dep, more):
            el = el_sb.rearrange("p b h -> p h b")
            W = H * NB
            tv = [tbl[:, i, 0:W].rearrange("p (h b) -> p h b", h=H) for i in range(3)]
            r = a0[:, 12700:12700 + W].rearrange("p (h b) -> p h b", h=H)
            v = V.do(lambda e: e.tensor_copy(tv[0], el), dep)
            v = V.do(lambda e: e.tensor_tensor(r, el, tv[0], ALU.subtract), v)
            v = V.do(lambda e: e.tensor_copy(tv[1], r), v)
            v = V.do(lambda e: e.tensor_tensor(r, r, tv[1], ALU.subtract), v)
            v_t = V.do(lambda e: e.tensor_copy(tv[2], r), v)
            NU = 4
            ot = a3[:, 3840:3840 + 640 * NU].bitcast(F8).rearrange("p (u n) -> p u n", u=NU)
            nb = small[:, 0:2 * W].bitcast(BF16).rearrange("p (t h b) -> p t h b", t=4, h=H)
            v_t = V.do(lambda e: e.tensor_scalar(nb, bc(ident[:, 0:100].rearrange("p (t o b) -> p t o b", t=4, o=1), [P, 4, H, NB]),
                                                 -BIG, None, ALU.mult), v_t)
            nbf = small[:, 0:2 * W].bitcast(BF16).rearrange("p (t w) -> p t w", t=4)
            per, stride = (4, 256) if H == 8 else (16, 32)
            of, pf = [dep] * NU, [v_t] * 3
            cnt, t_last = [0], [None]

            def part(g, u, q, m, l):
                b = cnt[0] % 3
                cnt[0] += 1
                pp = pbig[b][:, 0:per * stride].rearrange("p (t w) -> p t w", w=stride)
                for i in range(m):
                    c = (q + i) // 4
                    T.do(lambda e, i=i, c=c: e.matmul(pp[:, i, 0:W], ot[0:100, u, 16 * P + P * c:16 * P + P * (c + 1)],
                                                      nbf[0:100, (q + i) % 4, :], start=True, stop=False), l, v_t, pf[b])
                    for k in range(3):
                        t = T.do(lambda e, i=i, k=k: e.matmul(pp[:, i, 0:W], ot[:, u, (q + i) * P:(q + i + 1) * P], tbl[:, k, 0:W],
                                                              start=False, stop=(k == 2)))
                j0 = 16 * g + q
                of[u] = t_last[0] = t
                pf[b] = V.do(lambda e: e.tensor_reduce(elv[:, j0:j0 + m, :], pp[:, 0:m, 0:W].rearrange("p t (h d) -> p t h d", d=NB), AX, ALU.max), t)

            def group(g):
                jn = min(16, J - 16 * g)
                u = g % NU
                l = land(f"ot{u}").go(S, lambda e: e.dma_start(ot[:, u, :], ot_d[:, GW * g:GW * (g + 1)]), of[u])
                for q in range(0, jn, per):
                    part(g, u, q, min(per, jn - q), l)
                    if more and more[0][0] <= 16 * g + q:
                        more.pop(0)[1]()

            for g in range(groups):
                group(g)
            return tuple(pf), t_last[0]

        def attention(H, eld, elsem, el_sb, hd, exd_flat, d, groups, look):
            elv = a0[:, 0:J * H].rearrange("p (j h) -> p j h", h=H)
            erv = a0[:, 6400:6400 + J * H].rearrange("p (j h) -> p j h", h=H)
            fv = a1f[:, 0:J * H].rearrange("p (j h) -> p j h", h=H)
            flat = [a0[:, 0:J * H], a0[:, 6400:6400 + J * H], a1f[:, 0:J * H]]
            K = {}
            more = []

            def later(col, f):
                more.append((col, f))

            def heads_in():
                K["l"] = land(f"hl{H}").go(S, lambda e: e.dma_start(flat[1], hd.rearrange("e h -> (e h)").rearrange("(p n) -> p n", p=P)), d)

            def er_sweep(first, h):
                def f():
                    K["e", first, h] = sweep(erv, erv, negh, h, -BIG if first else cin[:, 0, h:h + 1])(*([K["l"]] if first else [K["ec"]]))
                return f

            def er_carry():
                K["ec"] = carry(erv, H, (0,), K["e", True, H - 1])

            def leaky_part(c0, c1):
                def f():
                    x, y = c0 * H, c1 * H
                    v = V.do(lambda e: e.tensor_tensor(flat[0][:, x:y], flat[0][:, x:y], flat[1][:, x:y], ALU.add),
                             K["e", False, H - 1], *K.get("done", (V.n and (V.sem, V.n),)))
                    K["lk"] = V.do(lambda e: e.scalar_tensor_tensor(out=flat[0][:, x:y], in0=flat[0][:, x:y], scalar=0.2, in1=flat[0][:, x:y],
                                                                    op0=ALU.mult, op1=ALU.max), v)
                return f

            def el_sweep(h, c0, c1):
                def f():
                    ini = fv[:, c0 - 1, h:h + 1] if c0 else -BIG
                    K["f", h] = sweep(fv, elv, negh, h, ini, False, c0, c1)(K.get(("f", h)), K["lk"])
                return f

            later(32 if H == 8 else 0, heads_in)
            c_er = 128 if H == 8 else 300
            for h in range(H):
                later(c_er, er_sweep(True, h))
            later(c_er, er_carry)
            for h in range(H):
                later(c_er, er_sweep(False, h))
            cuts = [240, 432, 544] if H == 8 else []
            for c0, c1 in zip([0] + cuts[:-1], cuts):
                later(c1, leaky_part(c0, c1))
                for h in range(H):
                    later(c1, el_sweep(h, c0, c1))
            toks, t_end = lookup(H, elv, el_sb, groups, look, more)
            while more:
                more.pop(0)[1]()
            g = None
            for j in range(16 * groups, J):
                g = land(f"eg{H}").go(G, lambda e, j=j: e.indirect_dma_start(
                    out=elv[:, j, :], out_offset=None, in_=eld,
                    in_offset=bass.IndirectOffsetOnAxis(ap=src_n[:, j:j + 1], axis=0)), elsem, d_src)
            V.need(*toks, g)
            K["done"] = toks
            c0 = cuts[-1] if cuts else 0
            leaky_part(c0, J)()
            for h in range(H):
                el_sweep(h, c0, J)()
            v = K["f", H - 1]
            for h in range(H):
                v = sweep(fv, fv, negt, h, -BIG, True)(v)
            v = carry(fv, H, (0, 1), v)
            for h in range(H):
                v2 = sweep(fv, fv, negh, h, cin[:, 0, h:h + 1])(v)
            for h in range(H):
                v = sweep(fv, fv, negt, h, cin[:, 1, h:h + 1], True)(v2)
            v2 = v
            hf = J * H // 2
            for x, y in ((0, hf), (hf, J * H)):
                v = V.do(lambda e, x=x, y=y: e.tensor_tensor(flat[2][:, x:y], flat[0][:, x:y], flat[2][:, x:y], ALU.subtract), v2)
                a = A.do(lambda e, x=x, y=y: e.activation(flat[2][:, x:y], flat[2][:, x:y], ACT.Exp), v)
                l = land(f"exs{H}").go(S, lambda e, x=x, y=y: e.dma_start(exd_flat[:, x:y], flat[2][:, x:y]), a)
            return l, K["lk"], (g, t_end), v

        S.need(c)
        d_ex, v_lk, v_free, v_sub = attention(8, el_d, d_el, elr[:, :, 0:8], h_d,
                            ex_d.rearrange("c p f -> (c p f)").rearrange("(p n) -> p n", p=P), R["sc"], 36, t2_land)
        acc1 = a0[:, :]
        z = V.do(lambda e: e.memset(acc1[:, 0:6400], 0.0), v_sub)
        G.need(*t2_ready, *v_free)
        tok = aggregate_heads(t2, acc1, d_ex, v_free[0], lambda: V.need(G.do(lambda e: e.memset(acc1[:, 6400:], 0.0), v_lk)))
        a13 = acc1.rearrange("p (b h w) -> p b h w", h=8, w=65)
        v = V.do(lambda e: e.tensor_scalar(den[:, :, :], a13[:, :, :, 64], 1e-30, None, ALU.max), tok)
        v = V.do(lambda e: e.reciprocal(den[:, :, :], den[:, :, :]), v)
        etmp = a3[:, 0:4096].rearrange("p (u n) -> p u n", n=512)
        v0 = v
        R = {}

        out_banks = (6, 7, 0, 1)

        def elu(b):
            u = 2 * (b % 4)
            blk = a13[:, b, :, 0:64]
            lo_ = etmp[:, u, :].rearrange("p (h d) -> p h d", h=8)
            v = V.do(lambda e: e.tensor_tensor(blk, blk, bc(den[:, b, :].rearrange("p (h o) -> p h o", o=1), [P, 8, 64]), ALU.mult), v0)
            v = V.do(lambda e: e.tensor_scalar(lo_, blk, 0.0, None, ALU.min), v, R.get(("y", b - 4)))
            R["x", b] = A.do(lambda e: e.activation(etmp[:, u + 1, :], etmp[:, u, :], ACT.Exp), v)

        def elu2(b):
            u = 2 * (b % 4)
            blk = a13[:, b, :, 0:64]
            o, x = (etmp[:, u + i, :].rearrange("p (h d) -> p h d", h=8) for i in range(2))
            R["o", b] = V.do(lambda e: e.scalar_tensor_tensor(out=o, in0=blk, scalar=0.0, in1=x, op0=ALU.max, op1=ALU.add), R["x", b])

        def turn2(b):
            R["y", b] = turn(etmp[:, 2 * (b % 4), :], 4, ysl(b % 2, 4), b % 2, R["o", b], -1.0)

        def product2(b):
            R["p", b] = multiply(ysl(b % 2, 4), b % 2, 4, gw2s, D + 2, R["y", b], out_banks[b % 4])

        def keep2(b):
            t = R["p", b]
            pb = out_banks[b % 4]
            a = A.do(lambda e: e.activation(a1[:, b, :], bank(pb)[:, 0:D], ACT.Copy), t)
            R["c"] = pfree[pb] = A.do(lambda e: e.activation(elr[:, b, 0:2], bank(pb)[:, D:D + 2], ACT.Copy), t)
            R["sc"] = starts(1, b, elr[:, b, 1:2], h2_d, R["c"])
            store(t3, "t3", b, a)

        pipeline((0, elu), (1, elu2), (2, turn2), (4, product2), (6, keep2))
        c = R["c"]
        d_t3 = land("t3").sem, land("t3").n
        d_el2 = land("el2").go(S, lambda e: e.dma_start(el2_d.rearrange("(b p) h -> p b h", p=P), elr[:, :, 0:1], allow_slow_non_contiguous=True), c)
        V.need(d_t3, c)
        G.need(c)
        d_ex2, v_lk, v_free, v_sub = attention(1, el2_d, d_el2, elr[:, :, 0:1], h2_d,
                             ex2_d.rearrange("c p -> (c p)").rearrange("(p n) -> p n", p=P), R["sc"], 44, d_t3)
        acc2 = a0[:, 0:NB * 257]
        z = V.do(lambda e: e.memset(acc2, 0.0), v_sub, v_lk)
        S.need(d_t3)
        G.need(d_t3, *v_free)
        V.do(lambda e: e.memset(a3[:, 0:SLOT * NR1].rearrange("p (r w) -> p r w", w=SLOT)[:, :, D:D + 1], 1.0), *v_free)
        xrow = a0[:, 8000:8896].rearrange("p (k w) -> p k w", k=7)

        def edge_weights():
            for k in range(7):
                r_in = land("rows").go(G, lambda e, k=k: e.indirect_dma_start(
                    out=xrow[:, k, :], out_offset=None, in_=ex2_d,
                    in_offset=bass.IndirectOffsetOnAxis(ap=smalli[:, 60 + k:61 + k], axis=0)), d_ex2)
            return to_slots(lambda k: xrow[:, k, :], r_in, wsl)

        tok = aggregate(t3, D + 1, acc2, z, ahead=v_free[0], weights=edge_weights)
        a23 = acc2.rearrange("p (b w) -> p b w", w=257)
        v = V.do(lambda e: e.tensor_scalar(deg[:, :], a23[:, :, 256], 1e-30, None, ALU.max), tok)
        v = V.do(lambda e: e.reciprocal(deg[:, :], deg[:, :]), v)
        v0 = v
        og = {}
        for b in range(NB):
            if b % 4 == 3:
                y = A.do(lambda e, b=b: e.activation(a1[:, b, :], a23[:, b, 0:D], ACT.Copy, scale=deg[:, b:b + 1]), v0)
                og[b] = G.do(lambda e, b=b: e.tensor_tensor(a1[:, b, :], a1[:, b, :], xres[:, b, :], ALU.add), y)
            else:
                og[b] = V.do(lambda e, b=b: e.scalar_tensor_tensor(out=a1[:, b, :], in0=a23[:, b, 0:D], scalar=deg[:, b:b + 1], in1=xres[:, b, :],
                                                                   op0=ALU.mult, op1=ALU.add), v0)
            if b < NB - 1 and b % 6 == 5:
                land("out").go(S, lambda e, b=b: e.dma_start(out[(b - 5) * P:(b + 1) * P, :].rearrange("(b p) n -> p b n", p=P),
                                                             a1[:, b - 5:b + 1, :]), *(og[i] for i in range(b - 5, b + 1)))
        fin = land("out").go(S, lambda e: e.dma_start(out[(NB - 1) * P:N, :], a1[0:LAST, NB - 1, :]), og[NB - 1])
        S.need(fin)

        block = ctx.enter_context(nc.Block())

        @block.sync
        def _(e):
            S.replay(e)

        @block.gpsimd
        def _(e):
            G.replay(e)

        @block.scalar
        def _(e):
            A.replay(e)

        @block.vector
        def _(e):
            V.replay(e)

        @block.tensor
        def _(e):
            T.replay(e)


_INS = ["x", "src", "dst", "edge_weight", "L0_gnn_W1", "L0_gnn_b1", "L0_gnn_g1", "L0_gnn_be1", "L0_gnn_W2", "L0_gnn_b2",
        "L0_gnn_g2", "L0_gnn_be2", "L0_gnn_Wp", "L0_gnn_bp", "L1_gnn_W1", "L1_gnn_attn_l1", "L1_gnn_attn_r1", "L1_gnn_W2",
        "L1_gnn_attn_l2", "L1_gnn_attn_r2"]
_OUTS = [((N, D), "float32")]


def kernel(**inputs):
    import numpy as _np
    import concourse.bacc as _bacc
    from concourse import mybir as _mybir
    from concourse.bass_utils import run_bass_kernel_spmd as _run

    nc = _bacc.Bacc("TRN2", target_bir_lowering=False, num_devices=1)
    arrays, args = {}, []
    for name in _INS:
        a = _np.ascontiguousarray(inputs[name])
        arrays[f"in_{name}_dram"] = a
        args.append(nc.dram_tensor(f"in_{name}_dram", a.shape, _mybir.dt.from_np(a.dtype), kind="ExternalInput").ap())
    for i, (shape, dtype) in enumerate(_OUTS):
        dt = _mybir.dt.from_np(_np.dtype(dtype))
        args.append(nc.dram_tensor(f"out_{i}_dram", shape, dt, kind="ExternalOutput").ap())
    program(nc, *args)
    r = _run(nc, [arrays], core_ids=[0])
    got = tuple(r.results[0][f"out_{i}_dram"] for i in range(len(_OUTS)))
    return got[0]
```
